# Optimizing a Trainium2 kernel written in Bass

```python
import numpy as np
import jax
import jax.numpy as jnp

def _softmax(x, axis=-1):
    return jax.nn.softmax(x, axis=axis)

def _gelu(x):
    return jax.nn.gelu(x, approximate=True)

def _silu(x):
    return jax.nn.silu(x)

def _sigmoid(x):
    return jax.nn.sigmoid(x)

def _layernorm(x, axis=-1, eps=1e-05):
    m = jnp.mean(x, axis=axis, keepdims=True)
    v = jnp.var(x, axis=axis, keepdims=True)
    return (x - m) / jnp.sqrt(v + eps)

def _scatter_add(tgt, idx, src, axis=0):
    return tgt.at[idx].add(src)

def _segment_sum(src, seg, n):
    return jax.ops.segment_sum(src, seg, n)
kernel_name = 'mk_cond_seq_d1_seqx_r2_fb68ff'

def setup_inputs(seed: int=0):
    np.random.seed(seed)
    _w = jnp.asarray

    def _rec_inputs():
        import jax
        import jax.numpy as jnp
        _rk = jax.random.key(seed)
        x = -0.0002928 + 1 * jax.random.normal(jax.random.fold_in(_rk, 1), (64, 128, 512), jnp.float32)
        _lenS = 128 - jax.random.randint(jax.random.fold_in(_rk, 7), (64,), 0, max(1, 128 // 4) + 1, jnp.int32)
        _lenS2 = 128 - jax.random.randint(jax.random.fold_in(_rk, 8), (64,), 0, max(1, 128 // 4) + 1, jnp.int32)
        cond_2048 = 0.0061147 + 1.02565 * jax.random.normal(jax.random.fold_in(_rk, 11), (64, 1024), jnp.float32)
        return (x, cond_2048)
    x, cond_2048 = _rec_inputs()

    def _L0_cond_setup():
        import jax, jax.numpy as jnp
        import numpy as np
        D = 512
        DI = 1024
        N = 16
        DT_RANK = 64
        D_CONV = 4
        EPS = 1e-05

        def _layernorm(x, g, b):
            mu = jnp.mean(x, axis=-1, keepdims=True)
            var = jnp.mean((x - mu) ** 2, axis=-1, keepdims=True)
            return (x - mu) * jax.lax.rsqrt(var + EPS) * g + b

        def _mamba(xn, in_proj_w, conv_w, conv_b, x_proj_w, dt_proj_w, dt_proj_b, A_log, D_param, out_proj_w):
            b, sl, _ = xn.shape
            xz = jnp.einsum('bsd,ed->bse', xn, in_proj_w)
            x_in, z = jnp.split(xz, 2, axis=-1)
            xt = jnp.transpose(x_in, (0, 2, 1))
            u = jax.lax.conv_general_dilated(xt, conv_w[:, None, :], (1,), [(D_CONV - 1, 0)], feature_group_count=DI, dimension_numbers=('NCH', 'OIH', 'NCH')) + conv_b[None, :, None]
            u = jax.nn.silu(jnp.transpose(u, (0, 2, 1)))
            x_dbl = jnp.einsum('bsd,ed->bse', u, x_proj_w)
            dt_r, B, C = jnp.split(x_dbl, [DT_RANK, DT_RANK + N], axis=-1)
            dt = jax.nn.softplus(jnp.einsum('bsr,dr->bsd', dt_r, dt_proj_w) + dt_proj_b)
            A = -jnp.exp(A_log)

            def step(h, inp):
                dt_t, B_t, C_t, u_t = inp
                dA = jnp.exp(dt_t[:, :, None] * A)
                h = h * dA + (dt_t * u_t)[:, :, None] * B_t[:, None, :]
                y = jnp.einsum('bdn,bn->bd', h, C_t)
                return (h, y)
            seq = (jnp.transpose(dt, (1, 0, 2)), jnp.transpose(B, (1, 0, 2)), jnp.transpose(C, (1, 0, 2)), jnp.transpose(u, (1, 0, 2)))
            h0 = jnp.zeros((b, DI, N), xn.dtype)
            _, ys = jax.lax.scan(step, h0, seq)
            y = jnp.transpose(ys, (1, 0, 2)) + u * D_param
            y = y * jax.nn.silu(z)
            return jnp.einsum('bsd,ed->bse', y, out_proj_w)
        key = jax.random.key(seed)
        ks = jax.random.split(key, 16)
        s = lambda fan: 1.0 / np.sqrt(fan)
        inp = {'x': jax.random.normal(ks[0], (2, 1024, D), jnp.float32), 'c': jax.random.normal(ks[1], (2, 2 * D), jnp.float32), 'ln_g': jnp.ones((D,), jnp.float32), 'ln_b': jnp.zeros((D,), jnp.float32), 'ada_w': jax.random.normal(ks[2], (3 * D, 2 * D), jnp.float32) * s(2 * D), 'ada_b': jnp.zeros((3 * D,), jnp.float32), 'in_proj_w': jax.random.normal(ks[3], (2 * DI, D), jnp.float32) * s(D), 'conv_w': jax.random.normal(ks[4], (DI, D_CONV), jnp.float32) * s(D_CONV), 'conv_b': jnp.zeros((DI,), jnp.float32), 'x_proj_w': jax.random.normal(ks[5], (DT_RANK + 2 * N, DI), jnp.float32) * s(DI), 'dt_proj_w': jax.random.normal(ks[6], (DI, DT_RANK), jnp.float32) * s(DT_RANK), 'dt_proj_b': jax.random.uniform(ks[7], (DI,), jnp.float32, -4.0, -2.0), 'A_log': jnp.tile(jnp.log(jnp.arange(1, N + 1, dtype=jnp.float32)), (DI, 1)), 'D_param': jnp.ones((DI,), jnp.float32), 'out_proj_w': jax.random.normal(ks[8], (D, DI), jnp.float32) * s(DI)}
        return inp
    _L0_cond_all = _L0_cond_setup()
    _L0_cond_in = {k: v for k, v in _L0_cond_all.items() if k in ('ln_g', 'ln_b', 'ada_w', 'ada_b', 'in_proj_w', 'conv_w', 'conv_b', 'x_proj_w', 'dt_proj_w', 'dt_proj_b', 'A_log', 'D_param', 'out_proj_w')}
    del _L0_cond_all
    return {'x': x, 'cond_2048': cond_2048, 'L0_cond_ln_g': _L0_cond_in['ln_g'], 'L0_cond_ln_b': _L0_cond_in['ln_b'], 'L0_cond_ada_w': _L0_cond_in['ada_w'], 'L0_cond_ada_b': _L0_cond_in['ada_b'], 'L0_cond_in_proj_w': _L0_cond_in['in_proj_w'], 'L0_cond_conv_w': _L0_cond_in['conv_w'], 'L0_cond_conv_b': _L0_cond_in['conv_b'], 'L0_cond_x_proj_w': _L0_cond_in['x_proj_w'], 'L0_cond_dt_proj_w': _L0_cond_in['dt_proj_w'], 'L0_cond_dt_proj_b': _L0_cond_in['dt_proj_b'], 'L0_cond_A_log': _L0_cond_in['A_log'], 'L0_cond_D_param': _L0_cond_in['D_param'], 'L0_cond_out_proj_w': _L0_cond_in['out_proj_w']}

def reference(x, cond_2048, L0_cond_ln_g, L0_cond_ln_b, L0_cond_ada_w, L0_cond_ada_b, L0_cond_in_proj_w, L0_cond_conv_w, L0_cond_conv_b, L0_cond_x_proj_w, L0_cond_dt_proj_w, L0_cond_dt_proj_b, L0_cond_A_log, L0_cond_D_param, L0_cond_out_proj_w):
    import jax
    import jax.numpy as jnp

    def _L0_cond_ref(x, c, ln_g, ln_b, ada_w, ada_b, in_proj_w, conv_w, conv_b, x_proj_w, dt_proj_w, dt_proj_b, A_log, D_param, out_proj_w):
        import jax, jax.numpy as jnp
        import numpy as np
        D = 512
        DI = 1024
        N = 16
        DT_RANK = 64
        D_CONV = 4
        EPS = 1e-05

        def _layernorm(x, g, b):
            mu = jnp.mean(x, axis=-1, keepdims=True)
            var = jnp.mean((x - mu) ** 2, axis=-1, keepdims=True)
            return (x - mu) * jax.lax.rsqrt(var + EPS) * g + b

        def _mamba(xn, in_proj_w, conv_w, conv_b, x_proj_w, dt_proj_w, dt_proj_b, A_log, D_param, out_proj_w):
            b, sl, _ = xn.shape
            xz = jnp.einsum('bsd,ed->bse', xn, in_proj_w)
            x_in, z = jnp.split(xz, 2, axis=-1)
            xt = jnp.transpose(x_in, (0, 2, 1))
            u = jax.lax.conv_general_dilated(xt, conv_w[:, None, :], (1,), [(D_CONV - 1, 0)], feature_group_count=DI, dimension_numbers=('NCH', 'OIH', 'NCH')) + conv_b[None, :, None]
            u = jax.nn.silu(jnp.transpose(u, (0, 2, 1)))
            x_dbl = jnp.einsum('bsd,ed->bse', u, x_proj_w)
            dt_r, B, C = jnp.split(x_dbl, [DT_RANK, DT_RANK + N], axis=-1)
            dt = jax.nn.softplus(jnp.einsum('bsr,dr->bsd', dt_r, dt_proj_w) + dt_proj_b)
            A = -jnp.exp(A_log)

            def step(h, inp):
                dt_t, B_t, C_t, u_t = inp
                dA = jnp.exp(dt_t[:, :, None] * A)
                h = h * dA + (dt_t * u_t)[:, :, None] * B_t[:, None, :]
                y = jnp.einsum('bdn,bn->bd', h, C_t)
                return (h, y)
            seq = (jnp.transpose(dt, (1, 0, 2)), jnp.transpose(B, (1, 0, 2)), jnp.transpose(C, (1, 0, 2)), jnp.transpose(u, (1, 0, 2)))
            h0 = jnp.zeros((b, DI, N), xn.dtype)
            _, ys = jax.lax.scan(step, h0, seq)
            y = jnp.transpose(ys, (1, 0, 2)) + u * D_param
            y = y * jax.nn.silu(z)
            return jnp.einsum('bsd,ed->bse', y, out_proj_w)
        ada = jnp.einsum('bc,ec->be', jax.nn.silu(c), ada_w) + ada_b
        shift, scale, gate = jnp.split(ada, 3, axis=1)
        xn = _layernorm(x, ln_g, ln_b)
        xn = xn * (1.0 + scale[:, None, :]) + shift[:, None, :]
        x_ssm = _mamba(xn, in_proj_w, conv_w, conv_b, x_proj_w, dt_proj_w, dt_proj_b, A_log, D_param, out_proj_w)
        return x + gate[:, None, :] * x_ssm
    x = _L0_cond_ref(x, cond_2048, L0_cond_ln_g, L0_cond_ln_b, L0_cond_ada_w, L0_cond_ada_b, L0_cond_in_proj_w, L0_cond_conv_w, L0_cond_conv_b, L0_cond_x_proj_w, L0_cond_dt_proj_w, L0_cond_dt_proj_b, L0_cond_A_log, L0_cond_D_param, L0_cond_out_proj_w)
    return x

_drawn_inputs = setup_inputs


def setup_inputs(seed=0):
    import zlib

    import numpy as np

    out = dict(_drawn_inputs(seed))
    spreads = {'L0_cond_ln_g': (1.0, 0.2),
     'L0_cond_ln_b': (0.0, 0.1),
     'L0_cond_ada_b': (0.0, 0.1),
     'L0_cond_conv_b': (0.0, 0.1),
     'L0_cond_D_param': (1.0, 0.2)}
    factors = {}
    for name, (base, spread) in spreads.items():
        noise = np.random.default_rng([zlib.crc32(name.encode()), seed]).standard_normal(out[name].shape)
        drawn = base * np.exp(spread * noise) if base else spread * noise
        out[name] = jnp.asarray(drawn.astype(out[name].dtype))
    for name, factor in factors.items():
        out[name] = (out[name] * factor).astype(out[name].dtype)
    return out
```

```python
from contextlib import ExitStack

import concourse.bass as bass
from concourse import mybir

P = 128


def mamba_block(nc, x, c_t, ln_g, ln_b, ada_wt, ada_b_col, ada_b_gate, in_wt, conv_w, conv_b, xproj_wt, dt_wt,
                dt_b, a_log, d_param, out_wt, eye, out):
    F32 = mybir.dt.float32
    ACT = mybir.ActivationFunctionType
    ALU = mybir.AluOpType

    B, S, D = x.shape
    DI = in_wt.shape[1] // 2
    RB = xproj_wt.shape[2]
    R = dt_wt.shape[0]
    N = (RB - R) // 2
    TAPS = conv_w.shape[2]
    KC = c_t.shape[0]
    BG = 2
    G = B // BG
    T = BG * S
    KD = D // P
    NC = DI // P
    HN = N // 2
    U = HN * T
    NH = 4
    EPS = 1e-5
    SILU_LOW = -40.0
    SOFTPLUS_HIGH = 30.0
    FRONT = {0: (0, 1), 1: (2, 3), 2: (4, 5), 3: (6, 7)}

    bc_dram = nc.dram_tensor("bc_rows", (2, 2 * N, T), F32, kind="Internal").ap()
    gate_dram = nc.dram_tensor("gate_rows", (B, D), F32, kind="Internal").ap()
    x_g = x.rearrange("(g b) t d -> g t b d", b=BG)
    out_g = out.rearrange("(g b) t d -> g t b d", b=BG)

    ctx = ExitStack()
    with ctx:
        def sb(name, shape):
            return ctx.enter_context(nc.sbuf_tensor(name, shape, F32))

        def sem(name):
            return ctx.enter_context(nc.semaphore(name))

        w_in = sb("w_in", [P, KD, 2 * DI])
        w_out = sb("w_out", [P, NC, D])
        w_x = sb("w_x", [P, NC, RB])
        w_dt = sb("w_dt", [P, DI])
        a_neg = sb("a_neg", [P, NC, N])
        cw = sb("cw", [P, NC, TAPS])
        cb = sb("cb", [P, NC])
        dtb = sb("dtb", [P, NC])
        dpar = sb("dpar", [P, NC])
        lng = sb("lng", [P, KD])
        lnb = sb("lnb", [P, KD])
        adb = sb("adb", [P, 2 * KD])
        ident = sb("ident", [P, P])
        eps_t = sb("eps_t", [P, 1])
        mod_a = sb("mod_a", [P, KD, B])
        mod_b = sb("mod_b", [P, KD, B])
        x_ln = sb("x_ln", [P, BG, D])
        st6 = sb("st6", [P, BG, 6])
        mv = sb("mv", [P, BG, 2])
        rstd = sb("rstd", [P, BG])
        xn = sb("xn", [P, 2, KD, T])
        acc = sb("acc", [P, 2, T])
        sig_u = sb("sig_u", [P, 2, T])
        u = sb("u", [P, 2, NC, T])
        xdbl = sb("xdbl", [P, 2, T])
        b_bc = sb("b_bc", [P, N, T])
        c_bc = sb("c_bc", [P, N, T])
        sp = sb("sp", [P, T])
        dt = sb("dt", [P, 2, T])
        xdt = sb("xdt", [P, 2, T])
        z_c = sb("z_c", [P, 2, T])
        sig_z = sb("sig_z", [P, 2, T])
        dec = sb("dec", [P, 2, HN, BG, S])
        h = sb("h", [P, NH, U])
        x_res = sb("x_res", [P, BG, D])
        gate = sb("gate", [P, BG, D])
        og = sb("og", [P, BG, D])

        pb = [ctx.enter_context(nc.psum_tensor(f"pb{i}", [P, 512], F32)) for i in range(8)]
        ps_in = pb[0:2]
        ps_dt = pb[2][:, 0:T]
        ps_z = pb[3][:, 0:T]
        ps_y = pb[4:6]
        ps_o = pb[6:8]
        ps_x = pb[0]

        b_flat = b_bc[:, :, :].rearrange("p n t -> p (n t)")
        c_flat = c_bc[:, :, :].rearrange("p n t -> p (n t)")
        h_flat = h[:, :, :].rearrange("p a n -> p (a n)")
        dec_flat = dec[:, :, :, :, :].rearrange("p a n b t -> p (a n b t)")
        ada_w = [flat[:, j * 3 * D:(j + 1) * 3 * D]
                 for flat in (b_flat, h_flat, dec_flat) for j in range(flat.shape[1] // (3 * D))][0:KC]

        used = [0]

        def lend(rows, n):
            used[0] += n
            return c_flat[0:rows, used[0] - n:used[0]]

        cond, cond_s = lend(P, KC * B), lend(P, KC * B)
        gate_bias, gate_rows = lend(B, D), lend(B, D)
        mod_t = lend(P, KD * B).rearrange("p (k b) -> p k b", k=KD)

        s_cond = sem("cond_loaded")
        s_small = sem("small_loaded")
        s_ada = sem("ada_loaded")
        s_wts = sem("weights_loaded")
        s_gb = sem("gate_bias_loaded")
        s_zeroed = sem("zeroed")
        s_eps = sem("eps_ready")
        s_cmin = sem("cond_clamped")
        s_csig = sem("cond_sigmoid_part")
        s_csilu = sem("cond_silu")
        s_ada_mm = sem("ada_products")
        s_gate_row = sem("gate_row_ready")
        s_gate_st = sem("gate_rows_stored")
        s_adb1 = sem("scale_bias_plus_one")
        s_modt = sem("mod_b_part")
        s_mod = sem("mod_ready")
        s_aexp = sem("a_exp")
        s_aneg = sem("a_neg_ready")
        s_xl = sem("x_loaded")
        s_st = sem("stats_taken")
        s_var = sem("var_ready")
        s_lnv = sem("ln_var")
        s_rstd = sem("rstd_ready")
        s_xhat = sem("xhat_ready")
        s_tr = sem("xhat_transposed")
        s_xn = sem("xn_ready")
        s_xin = sem("in_proj_x")
        s_acc = sem("conv_started")
        s_tap = sem("conv_tap")
        s_conv = sem("conv_ready")
        s_sgu = sem("sigmoid_u_part")
        s_sigu = sem("sigmoid_u")
        s_u = sem("u_ready")
        s_xp = sem("x_proj")
        s_xd = sem("xdbl_ready")
        s_bcst = sem("bc_rows_stored")
        s_bl = [sem(f"b_loaded{k}") for k in range(2)]
        s_cl = [sem(f"c_loaded{k}") for k in range(2)]
        s_dtp = sem("dt_proj")
        s_q = sem("softplus_clamped")
        s_e = sem("softplus_exp")
        s_l = sem("softplus_log")
        s_dt = sem("dt_ready")
        s_xdt = sem("xdt_ready")
        s_dec = sem("decay_ready")
        s_dbu = sem("input_term_ready")
        s_scan = sem("states_ready")
        s_hc = sem("weighted_states_ready")
        s_y = sem("y_unit_summed")
        s_z = sem("in_proj_z")
        s_zc = sem("z_clamped")
        s_sgz = sem("sigmoid_z_part")
        s_sigz = sem("sigmoid_z")
        s_w = sem("silu_z")
        s_yd = sem("y_with_skip")
        s_yz = sem("gated_y_ready")
        s_gl = sem("gate_loaded")
        s_xrl = sem("x_res_loaded")
        s_oc = sem("out_proj_chunk")
        s_og = sem("gated_out")
        s_res = sem("result_ready")
        s_out = sem("result_stored")

        def need(eng, s, v):
            if not (isinstance(v, int) and v <= 0):
                eng.wait_ge(s, v)

        def exists(g):
            return not (isinstance(g, int) and g >= G)

        def later(g, c, k):
            return g + (c + k) // NC, (c + k) // NC, (c + k) % NC

        def over_groups(eng, step):
            for g in (0, 1):
                for c in range(NC):
                    step(g, g % 2, c)
            with eng.Fori(1, G // 2 - 1) as i:
                for half in (0, 1):
                    for c in range(NC):
                        step(2 * i + half, half, c)
            for g in (G - 2, G - 1):
                for c in range(NC):
                    step(g, g % 2, c)

        block = ctx.enter_context(nc.Block())

        @block.sync
        def _(eng):
            def load_x(g):
                eng.dma_start(x_ln[:, :, :], x_g[g]).then_inc(s_xl, 16)

            def store_bc(g, par):
                need(eng, s_xd, g + 1)
                eng.dma_start(bc_dram[par], xdbl[R:RB, par, :]).then_inc(s_bcst, 16)
                eng.wait_ge(s_bcst, 16 * (g + 1))

            def spread(dst, par, row, done):
                rows = bc_dram[par, row:row + HN, :].rearrange("n t -> (n t)")[None, :]
                eng.dma_start(dst.rearrange("p n t -> p (n t)"), rows.to_broadcast([P, U])).then_inc(done, 16)

            def load_b(par, k):
                spread(b_bc[:, k * HN:(k + 1) * HN, :], par, k * HN, s_bl[k])

            def load_c(par, k):
                spread(c_bc[:, k * HN:(k + 1) * HN, :], par, N + k * HN, s_cl[k])

            def load_out_operands(g):
                eng.dma_start(x_res[:, :, :], x_g[g]).then_inc(s_xrl, 16)
                rows = gate_g[g][None, :]
                eng.dma_start(gate[:, :, :].rearrange("p b d -> p (b d)"),
                              rows.to_broadcast([P, BG * D])).then_inc(s_gl, 16)

            def store_out(g):
                need(eng, s_res, BG * (g + 1))
                eng.dma_start(out_g[g], x_res[:, :, :]).then_inc(s_out, 16)
                need(eng, s_out, 16 * (g + 1))

            gate_g = gate_dram.rearrange("(g b) d -> g (b d)", b=BG)

            eng.dma_start(cond, c_t.rearrange("k p b -> p k b")).then_inc(s_cond, 16)
            load_x(0)
            small = [(ident[:, :], eye), (a_neg[:, :, :], a_log), (cw[:, :, :], conv_w), (cb[:, :], conv_b),
                     (dtb[:, :], dt_b), (dpar[:, :], d_param), (lng[:, :], ln_g), (lnb[:, :], ln_b),
                     (adb[:, :], ada_b_col), (w_x[:, :, :], xproj_wt.rearrange("k p r -> p k r")),
                     (w_dt[0:R, :], dt_wt)]
            assert len(small) == SMALL
            for dst, src in small:
                eng.dma_start(dst, src).then_inc(s_small, 16)
            eng.dma_start(gate_bias, ada_b_gate.to_broadcast([B, D])).then_inc(s_gb, 16)
            for k in range(KC):
                eng.dma_start(ada_w[k], ada_wt[k]).then_inc(s_ada, 16)
            eng.dma_start(w_in[:, :, :], in_wt.rearrange("(k p) e -> p k e", p=P)).then_inc(s_wts, 16)
            eng.dma_start(w_out[:, :, :], out_wt.rearrange("(k p) e -> p k e", p=P)).then_inc(s_wts, 16)
            eng.wait_ge(s_gate_row, 1)
            eng.dma_start(gate_dram, gate_rows).then_inc(s_gate_st, 16)
            eng.wait_ge(s_gate_st, 16)
            eng.wait_ge(s_mod, 2)
            eng.wait_ge(s_tr, KD)
            load_x(1)
            store_bc(0, 0)
            for k in range(2):
                load_b(0, k)
                load_c(0, k)
            load_out_operands(0)

            def step(g, par, c):
                if c == 0 and exists(g + 2):
                    need(eng, s_tr, KD * (g + 2))
                    load_x(g + 2)
                if c == 3 and not (isinstance(g, int) and g == 0):
                    store_out(g - 1)
                    need(eng, s_og, BG * g)
                    load_out_operands(g)
                if c == 6 and exists(g + 1):
                    store_bc(g + 1, 1 - par)
                if c == 7 and exists(g + 1):
                    for k in range(2):
                        need(eng, s_dbu, 2 * (NC * g + c) + k + 1)
                        load_b(1 - par, k)
                        need(eng, s_hc, 2 * (NC * g + c) + k + 1)
                        load_c(1 - par, k)

            over_groups(eng, step)
            store_out(G - 1)

        @block.tensor
        def _(pe):
            def transposes(g):
                need(pe, s_xhat, BG * (g + 1))
                need(pe, s_conv, NC * g)
                need(pe, s_xd, g)
                for k in range(KD):
                    for b in range(BG):
                        last = nc.tensor.transpose(ps_in[k // 2][:, (k % 2) * T + b * S:(k % 2) * T + (b + 1) * S],
                                                   x_ln[:, b, k * P:(k + 1) * P], ident[:, :])
                    last.then_inc(s_tr, 1)

            def in_proj_x(g, par, e):
                if e == 0:
                    need(pe, s_xn, BG * KD * (g + 1))
                if e >= 2:
                    need(pe, s_conv, NC * g + e - 1)
                for k in range(KD):
                    last = nc.tensor.matmul(ps_in[e % 2][:, 0:T], w_in[:, k, e * P:(e + 1) * P], xn[:, par, k, :],
                                            start=(k == 0), stop=(k == KD - 1))
                last.then_inc(s_xin, 1)

            def x_proj(g, par):
                need(pe, s_conv, NC * (g + 1))
                need(pe, s_u, NC * (g + 1))
                for e in range(NC):
                    last = nc.tensor.matmul(ps_x[0:RB, 0:T], w_x[:, e, :], u[:, par, e, :],
                                            start=(e == 0), stop=(e == NC - 1))
                last.then_inc(s_xp, 1)

            def dt_proj(g, par, c):
                if c == 0:
                    need(pe, s_xd, g + 1)
                need(pe, s_dt, NC * g + c)
                nc.tensor.matmul(ps_dt, w_dt[:, c * P:(c + 1) * P], xdbl[:, par, :],
                                 start=True, stop=True).then_inc(s_dtp, 1)

            def in_proj_z(g, par, c):
                need(pe, s_zc, NC * g + c)
                for k in range(KD):
                    last = nc.tensor.matmul(ps_z, w_in[:, k, DI + c * P:DI + (c + 1) * P], xn[:, par, k, :],
                                            start=(k == 0), stop=(k == KD - 1))
                last.then_inc(s_z, 1)

            def sum_states(g, c, k):
                need(pe, s_hc, 2 * (NC * g + c) + k + 1)
                if k == 0:
                    need(pe, s_yd, NC * g + c - 1)
                for n in range(HN):
                    last = nc.tensor.matmul(ps_y[c % 2][:, 0:T], ident[:, :],
                                            h[:, (2 * c + k) % NH, n * T:(n + 1) * T],
                                            start=(k == 0 and n == 0), stop=(k == 1 and n == HN - 1))
                last.then_inc(s_y, 1)

            def out_proj(g, par, c):
                need(pe, s_yz, NC * g + c + 1)
                if c == 0:
                    need(pe, s_og, BG * g)
                for b in range(BG):
                    last = nc.tensor.matmul(ps_o[b][:, 0:D], u[:, par, c, b * S:(b + 1) * S], w_out[:, c, :],
                                            start=(c == 0), stop=(c == NC - 1))
                last.then_inc(s_oc, 1)

            pe.wait_ge(s_csilu, 1)
            pe.wait_ge(s_ada, 16 * KC)
            for m in range(2 * KD):
                for k in range(KC):
                    last = nc.tensor.matmul(ps_in[0][:, m * B:(m + 1) * B], ada_w[k][:, m * P:(m + 1) * P],
                                            cond_s[:, k * B:(k + 1) * B], start=(k == 0), stop=(k == KC - 1))
            last.then_inc(s_ada_mm, 1)
            for k in range(KC):
                last = nc.tensor.matmul(ps_o[0][0:B, 0:D], cond_s[:, k * B:(k + 1) * B],
                                        ada_w[k][:, 2 * D:3 * D], start=(k == 0), stop=(k == KC - 1))
            last.then_inc(s_ada_mm, 1)
            pe.wait_ge(s_small, 16 * SMALL)
            pe.wait_ge(s_mod, 2)
            transposes(0)
            pe.wait_ge(s_wts, 32)
            for e in range(NC):
                in_proj_x(0, 0, e)
            x_proj(0, 0)
            pe.wait_ge(s_zeroed, 1)
            dt_proj(0, 0, 0)
            in_proj_z(0, 0, 0)
            transposes(1)
            dt_proj(0, 0, 1)
            pe.wait_ge(s_gate_row, 1)

            def step(g, par, c):
                if exists(g + 1):
                    if c == 5:
                        x_proj(g + 1, 1 - par)
                    for e in FRONT.get(c, ()):
                        in_proj_x(g + 1, 1 - par, e)
                g2, flip, c2 = later(g, c, 2)
                if exists(g2):
                    dt_proj(g2, par ^ flip, c2)
                sum_states(g, c, 0)
                g1, flip, c1 = later(g, c, 1)
                if exists(g1):
                    in_proj_z(g1, par ^ flip, c1)
                if c == 7 and exists(g + 2):
                    transposes(g + 2)
                if not (isinstance(g, int) and g == 0 and c < 2):
                    gm, flip, cm = later(g, c, -2)
                    out_proj(gm, par ^ (flip & 1), cm)
                sum_states(g, c, 1)

            over_groups(pe, step)
            for c in (NC - 2, NC - 1):
                out_proj(G - 1, 1, c)

        @block.scalar
        def _(act):
            def sigmoid(src, dst, part, done, count):
                nc.scalar.activation(dst, src, ACT.Exp, scale=-1.0).then_inc(part, 1)
                need(act, part, 2 * count + 1)
                nc.scalar.activation(dst, dst, ACT.Ln, bias=1.0).then_inc(part, 1)
                need(act, part, 2 * count + 2)
                nc.scalar.activation(dst, dst, ACT.Exp, scale=-1.0).then_inc(done, 1)

            def rstd_of(g):
                need(act, s_var, g + 1)
                nc.scalar.activation(rstd[:, :], mv[:, :, 1], ACT.Ln, bias=eps_t[:, 0:1]).then_inc(s_lnv, 1)
                need(act, s_lnv, g + 1)
                nc.scalar.activation(rstd[:, :], rstd[:, :], ACT.Exp, scale=-0.5).then_inc(s_rstd, 1)

            def modulate(g, par):
                need(act, s_z, NC * (g - 1))
                for k in range(KD):
                    need(act, s_tr, KD * g + k // 2 * 2 + 2)
                    for b in range(BG):
                        nc.scalar.activation(
                            xn[:, par, k, b * S:(b + 1) * S],
                            ps_in[k // 2][:, (k % 2) * T + b * S:(k % 2) * T + (b + 1) * S], ACT.Identity,
                            scale=mod_col(mod_a, k, g, b), bias=mod_col(mod_b, k, g, b)).then_inc(s_xn, 1)

            def mod_col(mod, k, g, b):
                return mod[:, k, bass.ds(g * BG + b, 1)]

            def start_conv(g, e):
                need(act, s_xin, NC * g + e + 1)
                need(act, s_u, NC * g + e - 1)
                nc.scalar.activation(acc[:, e % 2, :], ps_in[e % 2][:, 0:T], ACT.Identity,
                                     scale=cw[:, e, TAPS - 1:TAPS], bias=cb[:, e:e + 1]).then_inc(s_acc, 1)

            def sigmoid_u(g, e):
                need(act, s_conv, NC * g + e + 1)
                sigmoid(acc[:, e % 2, :], sig_u[:, e % 2, :], s_sgu, s_sigu, NC * g + e)

            def xdbl_out(g, par):
                need(act, s_xp, g + 1)
                need(act, s_bcst, 16 * (g - 1))
                need(act, s_dtp, NC * (g - 1))
                nc.scalar.activation(xdbl[0:RB, par, :], ps_x[0:RB, 0:T], ACT.Copy).then_inc(s_xd, 1)

            def softplus(g, c):
                s = NC * g + c
                need(act, s_q, s + 1)
                nc.scalar.activation(sp[:, :], sp[:, :], ACT.Exp).then_inc(s_e, 1)
                need(act, s_e, s + 1)
                nc.scalar.activation(sp[:, :], sp[:, :], ACT.Ln, bias=1.0).then_inc(s_l, 1)

            def decays(g, c, k):
                s = NC * g + c
                need(act, s_dt, s + 1)
                need(act, s_scan, 2 * s + k - 1)
                for n in range(HN):
                    last = nc.scalar.activation(
                        dec[:, k, n, :, 1:S], dt[:, c % 2, :].rearrange("p (b t) -> p b t", b=BG)[:, :, 1:S],
                        ACT.Exp, scale=a_neg[:, c, k * HN + n:k * HN + n + 1])
                last.then_inc(s_dec, 1)

            def sigmoid_of_z(g, c):
                s = NC * g + c
                need(act, s_zc, s + 1)
                need(act, s_yz, s - 1)
                sigmoid(z_c[:, c % 2, :], sig_z[:, c % 2, :], s_sgz, s_sigz, s)

            nc.scalar.preload_act_table_set("natural_log_exp_and_others")
            act.wait_ge(s_cmin, 1)
            sigmoid(cond, cond_s, s_csig, s_csig, 0)
            act.wait_ge(s_small, 16 * SMALL)
            nc.scalar.activation(a_neg[:, :, :], a_neg[:, :, :], ACT.Exp).then_inc(s_aexp, 1)
            act.wait_ge(s_aexp, 1)
            nc.scalar.activation(a_neg[:, :, :], a_neg[:, :, :], ACT.Copy, scale=-1.0).then_inc(s_aneg, 1)
            act.wait_ge(s_eps, 1)
            rstd_of(0)
            act.wait_ge(s_mod, 2)
            modulate(0, 0)
            for e in range(NC):
                start_conv(0, e)
                if e:
                    sigmoid_u(0, e - 1)
            sigmoid_u(0, NC - 1)
            xdbl_out(0, 0)
            rstd_of(1)
            softplus(0, 0)
            act.wait_ge(s_aneg, 1)
            act.wait_ge(s_zeroed, 1)
            decays(0, 0, 0)
            decays(0, 0, 1)

            def step(g, par, c):
                g1, flip, c1 = later(g, c, 1)
                if exists(g1):
                    softplus(g1, c1)
                conv = FRONT.get(c - 1, ()) if exists(g + 1) else ()
                for e in conv:
                    start_conv(g + 1, e)
                if exists(g1):
                    decays(g1, c1, 0)
                if c == 0 and exists(g + 1):
                    modulate(g + 1, 1 - par)
                for e in conv:
                    sigmoid_u(g + 1, e)
                if exists(g1):
                    decays(g1, c1, 1)
                sigmoid_of_z(g, c)
                if c == 6 and exists(g + 2):
                    rstd_of(g + 2)
                if c == 5 and exists(g + 1):
                    xdbl_out(g + 1, 1 - par)

            over_groups(act, step)

        @block.vector
        def _(dve):
            v = nc.vector

            def statistics(g):
                need(dve, s_xl, 16 * (g + 1))
                for b in range(BG):
                    last = v.bn_stats(st6[:, b, :], x_ln[:, b, :])
                last.then_inc(s_st, 1)

            def aggregate():
                for b in range(BG):
                    last = v.bn_aggr(mv[:, b, :], st6[:, b, :])
                last.then_inc(s_var, 1)

            def normalize(g):
                need(dve, s_var, g + 1)
                need(dve, s_rstd, g + 1)
                for b in range(BG):
                    v.tensor_scalar(x_ln[:, b, :], x_ln[:, b, :], mv[:, b, 0:1], rstd[:, b:b + 1],
                                    ALU.subtract, ALU.mult).then_inc(s_xhat, 1)

            def convolve(g, e):
                count = NC * g + e
                need(dve, s_acc, count + 1)
                src = ps_in[e % 2][:, 0:T].rearrange("p (b t) -> p b t", b=BG)
                dst = acc[:, e % 2, :].rearrange("p (b t) -> p b t", b=BG)
                for j in range(1, TAPS):
                    v.scalar_tensor_tensor(out=dst[:, :, j:S], in0=src[:, :, 0:S - j],
                                           scalar=cw[:, e, TAPS - 1 - j:TAPS - j], in1=dst[:, :, j:S],
                                           op0=ALU.mult, op1=ALU.add).then_inc(s_tap, 1)
                    need(dve, s_tap, (TAPS - 1) * count + j)
                v.tensor_scalar(acc[:, e % 2, :], acc[:, e % 2, :], SILU_LOW, None, ALU.max).then_inc(s_conv, 1)

            def clamp_dt(g, c):
                need(dve, s_dtp, NC * g + c + 1)
                need(dve, s_dt, NC * g + c)
                v.tensor_scalar(sp[:, :], ps_dt, dtb[:, c:c + 1], SOFTPLUS_HIGH,
                                ALU.add, ALU.min).then_inc(s_q, 1)

            def make_dt(g, c, par):
                s = NC * g + c
                need(dve, s_l, s + 1)
                need(dve, s_dec, 2 * s - 2)
                v.scalar_tensor_tensor(out=dt[:, c % 2, :], in0=ps_dt, scalar=dtb[:, c:c + 1], in1=sp[:, :],
                                       op0=ALU.add, op1=ALU.max).then_inc(s_dt, 1)
                need(dve, s_dt, s + 1)
                need(dve, s_u, s + 1)
                v.tensor_tensor(xdt[:, c % 2, :], dt[:, c % 2, :], u[:, par, c, :], ALU.mult).then_inc(s_xdt, 1)

            def scan_unit(g, c, k):
                s = NC * g + c
                unit = 2 * s + k
                hb = h[:, (2 * c + k) % NH, :]
                need(dve, s_xdt, s + 1)
                if c == 0:
                    need(dve, s_bl[k], 16 * (g + 1))
                need(dve, s_y, unit - NH + 1)
                v.tensor_tensor(hb.rearrange("p (n t) -> p n t", n=HN),
                                xdt[:, c % 2, :][:, None, :].to_broadcast([P, HN, T]),
                                b_bc[:, k * HN:(k + 1) * HN, :], ALU.mult).then_inc(s_dbu, 1)
                need(dve, s_dbu, unit + 1)
                need(dve, s_dec, unit + 1)
                v.tensor_tensor_scan(hb, dec[:, k, :, :, :].rearrange("p n b t -> p (n b t)"), hb, 0.0,
                                     ALU.mult, ALU.add).then_inc(s_scan, 1)

            def clamp_z(g, c):
                s = NC * g + c
                need(dve, s_z, s + 1)
                need(dve, s_w, s - 1)
                v.tensor_scalar(z_c[:, c % 2, :], ps_z, SILU_LOW, None, ALU.max).then_inc(s_zc, 1)

            def skip(g, c, par):
                s = NC * g + c
                need(dve, s_y, 2 * s + 2)
                v.scalar_tensor_tensor(out=u[:, par, c, :], in0=u[:, par, c, :], scalar=dpar[:, c:c + 1],
                                       in1=ps_y[c % 2][:, 0:T], op0=ALU.mult, op1=ALU.add).then_inc(s_yd, 1)

            def apply_gate(g):
                need(dve, s_gl, 16 * (g + 1))
                need(dve, s_oc, NC * (g + 1))
                for b in range(BG):
                    need(dve, s_res, BG * (g - 1) + b + 1)
                    v.tensor_tensor(og[:, b, :], gate[:, b, :], ps_o[b][:, 0:D], ALU.mult).then_inc(s_og, 1)

            v.memset(eps_t[:, :], EPS).then_inc(s_eps, 1)
            dve.wait_ge(s_cond, 16)
            v.tensor_scalar(cond, cond, SILU_LOW, None, ALU.max).then_inc(s_cmin, 1)
            v.memset(w_dt[R:P, :], 0.0)
            v.memset(xdbl[RB:P, :, :], 0.0)
            statistics(0)
            dve.wait_ge(s_st, 1)
            aggregate()
            dve.wait_ge(s_csig, 3)
            dve.wait_ge(s_cmin, 1)
            v.tensor_tensor(cond_s, cond_s, cond, ALU.mult).then_inc(s_csilu, 1)
            dve.wait_ge(s_small, 16 * SMALL)
            v.tensor_scalar(adb[:, KD:2 * KD], adb[:, KD:2 * KD], 1.0, None, ALU.add).then_inc(s_adb1, 1)
            normalize(0)
            dve.wait_ge(s_ada_mm, 1)
            dve.wait_ge(s_adb1, 1)
            for k in range(KD):
                scale = ps_in[0][:, (KD + k) * B:(KD + k + 1) * B]
                v.tensor_scalar(mod_t[:, k, :], scale, adb[:, KD + k:KD + k + 1], lnb[:, k:k + 1],
                                ALU.add, ALU.mult).then_inc(s_modt, 1)
                last = v.tensor_scalar(mod_a[:, k, :], scale, adb[:, KD + k:KD + k + 1], lng[:, k:k + 1],
                                       ALU.add, ALU.mult)
            last.then_inc(s_mod, 1)
            dve.wait_ge(s_modt, KD)
            for k in range(KD):
                last = v.scalar_tensor_tensor(out=mod_b[:, k, :], in0=ps_in[0][:, k * B:(k + 1) * B],
                                              scalar=adb[:, k:k + 1], in1=mod_t[:, k, :], op0=ALU.add, op1=ALU.add)
            last.then_inc(s_mod, 1)
            dve.wait_ge(s_ada_mm, 2)
            dve.wait_ge(s_gb, 16)
            v.tensor_tensor(gate_rows, gate_bias, ps_o[0][0:B, 0:D], ALU.add).then_inc(s_gate_row, 1)
            v.memset(dec_flat, 0.0).then_inc(s_zeroed, 1)
            for e in range(NC):
                convolve(0, e)
            statistics(1)
            dve.wait_ge(s_st, 2)
            aggregate()
            clamp_dt(0, 0)
            make_dt(0, 0, 0)
            normalize(1)

            def step(g, par, c):
                g1, flip, c1 = later(g, c, 1)
                if exists(g1):
                    clamp_dt(g1, c1)
                scan_unit(g, c, 0)
                if exists(g1):
                    make_dt(g1, c1, par ^ flip)
                if exists(g + 1):
                    for e in FRONT.get(c - 1, ()):
                        convolve(g + 1, e)
                if exists(g + 2) and c == 6:
                    statistics(g + 2)
                if exists(g + 2) and c == 7:
                    normalize(g + 2)
                if c == 2 and not (isinstance(g, int) and g == 0):
                    apply_gate(g - 1)
                scan_unit(g, c, 1)
                if c == 6 and exists(g + 2):
                    need(dve, s_st, g + 3)
                clamp_z(g, c)
                if c == 6 and exists(g + 2):
                    aggregate()
                if c:
                    skip(g, c - 1, par)
                elif not (isinstance(g, int) and g == 0):
                    skip(g - 1, NC - 1, 1 - par)

            over_groups(dve, step)
            skip(G - 1, NC - 1, 1)
            apply_gate(G - 1)

        @block.gpsimd
        def _(pool):
            def weight_states(g, c, k):
                unit = 2 * (NC * g + c) + k
                hb = h[:, (2 * c + k) % NH, :]
                if c == 0:
                    need(pool, s_cl[k], 16 * (g + 1))
                need(pool, s_scan, unit + 1)
                nc.gpsimd.tensor_tensor(hb, hb, c_bc[:, k * HN:(k + 1) * HN, :].rearrange("p n t -> p (n t)"),
                                        ALU.mult).then_inc(s_hc, 1)

            def make_u(g, par, e):
                need(pool, s_sigu, NC * g + e + 1)
                need(pool, s_oc, NC * (g - 2) + e + 1)
                nc.gpsimd.tensor_tensor(u[:, par, e, :], acc[:, e % 2, :], sig_u[:, e % 2, :],
                                        ALU.mult).then_inc(s_u, 1)

            def silu_z(g, c):
                need(pool, s_sigz, NC * g + c + 1)
                nc.gpsimd.tensor_tensor(sig_z[:, c % 2, :], sig_z[:, c % 2, :], z_c[:, c % 2, :],
                                        ALU.mult).then_inc(s_w, 1)

            def gate_y(g, par, c):
                s = NC * g + c
                need(pool, s_w, s + 1)
                need(pool, s_yd, s + 1)
                nc.gpsimd.tensor_tensor(u[:, par, c, :], u[:, par, c, :], sig_z[:, c % 2, :],
                                        ALU.mult).then_inc(s_yz, 1)

            def add_residual(g):
                need(pool, s_xrl, 16 * (g + 1))
                for b in range(BG):
                    need(pool, s_og, BG * g + b + 1)
                    nc.gpsimd.tensor_tensor(x_res[:, b, :], x_res[:, b, :], og[:, b, :],
                                            ALU.add).then_inc(s_res, 1)

            for e in range(NC):
                make_u(0, 0, e)

            def step(g, par, c):
                weight_states(g, c, 0)
                first = isinstance(g, int) and g == 0 and c == 0
                gp, flip, cp = later(g, c, -1)
                if not first:
                    silu_z(gp, cp)
                weight_states(g, c, 1)
                if exists(g + 1):
                    for e in FRONT.get(c - 1, ()):
                        make_u(g + 1, 1 - par, e)
                if not first:
                    gate_y(gp, par ^ (flip & 1), cp)
                if c == 3 and not (isinstance(g, int) and g == 0):
                    add_residual(g - 1)

            over_groups(pool, step)
            silu_z(G - 1, NC - 1)
            gate_y(G - 1, 1, NC - 1)
            add_residual(G - 1)


SMALL = 11


def columns(vector, parts):
    return vector.reshape(parts, P).T


def kernel(x, cond_2048, L0_cond_ln_g, L0_cond_ln_b, L0_cond_ada_w, L0_cond_ada_b, L0_cond_in_proj_w, L0_cond_conv_w,
           L0_cond_conv_b, L0_cond_x_proj_w, L0_cond_dt_proj_w, L0_cond_dt_proj_b, L0_cond_A_log, L0_cond_D_param,
           L0_cond_out_proj_w):
    import numpy as np
    import concourse.bacc as bacc
    from concourse.bass_utils import run_bass_kernel_spmd

    (x, cond, ln_g, ln_b, ada_w, ada_b, in_w, conv_w, conv_b, x_w, dt_w, dt_b, a_log, d_param, out_w) = [
        np.asarray(a) for a in
        (x, cond_2048, L0_cond_ln_g, L0_cond_ln_b, L0_cond_ada_w, L0_cond_ada_b, L0_cond_in_proj_w, L0_cond_conv_w,
         L0_cond_conv_b, L0_cond_x_proj_w, L0_cond_dt_proj_w, L0_cond_dt_proj_b, L0_cond_A_log, L0_cond_D_param,
         L0_cond_out_proj_w)]
    D, DI = x.shape[2], in_w.shape[0] // 2
    kd, nch, kc = D // P, DI // P, cond.shape[1] // P
    arrays = {
        "x": x,
        "c_t": cond.T.reshape(kc, P, cond.shape[0]),
        "ln_g": columns(ln_g, kd),
        "ln_b": columns(ln_b, kd),
        "ada_wt": ada_w.T.reshape(kc, P, 3 * D),
        "ada_b_col": columns(ada_b[0:2 * D], 2 * kd),
        "ada_b_gate": ada_b[2 * D:].reshape(1, D),
        "in_wt": in_w.T,
        "conv_w": conv_w.reshape(nch, P, -1).transpose(1, 0, 2),
        "conv_b": columns(conv_b, nch),
        "xproj_wt": x_w.T.reshape(nch, P, -1),
        "dt_wt": dt_w.T,
        "dt_b": columns(dt_b, nch),
        "a_log": a_log.reshape(nch, P, -1).transpose(1, 0, 2),
        "d_param": columns(d_param, nch),
        "out_wt": out_w.T,
        "eye": np.eye(P, dtype=np.float32),
    }
    arrays = {name: np.ascontiguousarray(a) for name, a in arrays.items()}
    nc = bacc.Bacc("TRN2", target_bir_lowering=False, num_devices=1)
    args = [nc.dram_tensor(name, a.shape, mybir.dt.from_np(a.dtype), kind="ExternalInput").ap()
            for name, a in arrays.items()]
    out = nc.dram_tensor("out", x.shape, mybir.dt.float32, kind="ExternalOutput").ap()
    mamba_block(nc, *args, out)
    got = run_bass_kernel_spmd(nc, [arrays], core_ids=[0])
    return got.results[0]["out"]
```

```python
from contextlib import ExitStack

import concourse.bass as bass
from concourse import mybir

P = 128


def mamba_block(nc, x, c_t, ln_g, ln_b, ada_wt, ada_b_col, ada_b_gate, in_wt, conv_w, conv_b, xproj_wt, dt_wt,
                dt_b, a_log, d_param, out_wt, eye, eye_blocks, out):
    F32 = mybir.dt.float32
    ACT = mybir.ActivationFunctionType
    ALU = mybir.AluOpType

    B, S, D = x.shape
    DI = in_wt.shape[1] // 2
    RB = xproj_wt.shape[2]
    R = dt_wt.shape[0]
    N = (RB - R) // 2
    TAPS = conv_w.shape[2]
    KC = c_t.shape[0]
    BG = 2
    G = B // BG
    T = BG * S
    KD = D // P
    NC = DI // P
    Q = 4
    CB = P // Q
    NB = P // CB
    QN = N // Q
    HN = QN // 2
    U = NB * HN * T
    NH = 4
    HALO = TAPS - 1
    EPS = 1e-5
    SILU_LOW = -40.0

    bc_dram = nc.dram_tensor("bc_rows", (2, 2 * N, T), F32, kind="Internal").ap()
    dtx_dram = nc.dram_tensor("dtx_rows", (2, CB, NB, 2 * T), F32, kind="Internal").ap()
    gate_dram = nc.dram_tensor("gate_rows", (B, D), F32, kind="Internal").ap()
    x_g = x.rearrange("(g b) t d -> g t b d", b=BG)
    out_g = out.rearrange("(g b) t d -> g t b d", b=BG)

    ctx = ExitStack()
    with ctx:
        def sb(name, shape):
            return ctx.enter_context(nc.sbuf_tensor(name, shape, F32))

        def sem(name):
            return ctx.enter_context(nc.semaphore(name))

        w_in = sb("w_in", [P, KD, 2 * DI])
        w_out = sb("w_out", [P, NC, D])
        w_x = sb("w_x", [P, NC, RB])
        w_dt = sb("w_dt", [P, DI])
        a_neg = sb("a_neg", [P, NC, NB, QN])
        cw = sb("cw", [P, NC, TAPS])
        cb = sb("cb", [P, NC])
        dpar = sb("dpar", [P, NC])
        lng = sb("lng", [P, KD])
        lnb = sb("lnb", [P, KD])
        adb = sb("adb", [P, 2 * KD])
        ident = sb("ident", [P, P])
        fold = sb("fold", [P, CB])
        taps = sb("taps", [P, NC, TAPS, P])
        eps_t = sb("eps_t", [P, 1])
        mod_a = sb("mod_a", [P, KD, B])
        mod_b = sb("mod_b", [P, KD, B])
        x_ln = sb("x_ln", [P, BG, D])
        st6 = sb("st6", [P, BG, 6])
        mv = sb("mv", [P, BG, 2])
        rstd = sb("rstd", [P, BG])
        xn = sb("xn", [P, KD, T])
        xz = sb("xz", [P, 2, KD, T])
        xs = sb("xs", [P, BG, HALO + S])
        acc = sb("acc", [P, T])
        sig_u = sb("sig_u", [P, T])
        u = sb("u", [P, 2, NC, T])
        xdbl = sb("xdbl", [P, T])
        b_bc = sb("b_bc", [P, QN, T])
        c_bc = sb("c_bc", [P, QN, T])
        sp = sb("sp", [P, T])
        dtx = sb("dtx", [P, 2, T])
        rep = sb("rep", [P, 2, NB, 2, T])
        z_c = sb("z_c", [P, 2, T])
        sig_z = sb("sig_z", [P, 2, T])
        dec = sb("dec", [P, 2, NB, HN, BG, S])
        h = sb("h", [P, NH, NB, HN, T])
        yz = sb("yz", [P, 2, T])
        x_res = sb("x_res", [P, BG, D])
        gate = sb("gate", [P, BG, D])

        pb = [ctx.enter_context(nc.psum_tensor(f"pb{i}", [P, 512], F32)) for i in range(8)]
        ps_in = pb[0]
        ps_cv = pb[1]
        ps_dt = pb[2][:, 0:T]
        ps_z = pb[3][:, 0:T]
        ps_y = pb[4:6]
        ps_o = pb[6:8]

        ada_w = [flat[:, j * 3 * D:(j + 1) * 3 * D]
                 for flat in (h[:, :, :, :, :].rearrange("p a c n t -> p (a c n t)"),
                              dec[:, :, :, :, :, :].rearrange("p a c n b t -> p (a c n b t)"),
                              u[:, :, :, :].rearrange("p a c t -> p (a c t)"))
                 for j in range(flat.shape[1] // (3 * D))][0:KC]
        rep_flat = rep[:, :, :, :, :].rearrange("p a c w t -> p (a c w t)")
        used = [0]

        def lend(rows, n):
            used[0] += n
            return rep_flat[0:rows, used[0] - n:used[0]]

        cond, cond_s = lend(P, KC * B), lend(P, KC * B)
        gate_bias, gate_rows = lend(B, D), lend(B, D)
        mod_t = lend(P, KD * B).rearrange("p (k b) -> p k b", k=KD)

        s_cond = sem("cond_loaded")
        s_small = sem("small_loaded")
        s_ada = sem("ada_loaded")
        s_win = sem("w_in_loaded")
        s_wout = sem("w_out_loaded")
        s_gb = sem("gate_bias_loaded")
        s_wdt = sem("w_dt_zeroed")
        s_dtb = sem("dt_bias_loaded")
        s_padded = sem("constant_parts_ready")
        s_zeroed = sem("zeroed")
        s_taps = sem("taps_ready")
        s_eps = sem("eps_ready")
        s_cmin = sem("cond_clamped")
        s_csig = sem("cond_sigmoid_part")
        s_csilu = sem("cond_silu")
        s_ada_mm = sem("ada_products")
        s_gate_row = sem("gate_row_ready")
        s_gate_st = sem("gate_rows_stored")
        s_adb1 = sem("scale_bias_plus_one")
        s_modt = sem("mod_b_part")
        s_mod = sem("mod_ready")
        s_aexp = sem("a_exp")
        s_aneg = sem("a_neg_ready")
        s_xl = sem("x_loaded")
        s_st = sem("stats_taken")
        s_var = sem("var_ready")
        s_lnv = sem("ln_var")
        s_rstd = sem("rstd_ready")
        s_xhat = sem("xhat_ready")
        s_tr = sem("xhat_transposed")
        s_xn = sem("xn_ready")
        s_xz = sem("xz_ready")
        s_xin = sem("in_proj_x")
        s_xs = sem("conv_input_ready")
        s_cv = sem("conv_products")
        s_uc = sem("conv_clamped")
        s_sgu = sem("sigmoid_u_part")
        s_sigu = sem("sigmoid_u")
        s_u = sem("u_ready")
        s_xp = sem("x_proj")
        s_xd = sem("xdbl_ready")
        s_bcst = sem("bc_rows_stored")
        s_bl = [sem(f"b_loaded{k}") for k in range(2)]
        s_cl = [sem(f"c_loaded{k}") for k in range(2)]
        s_dtp = sem("dt_proj")
        s_abs = sem("softplus_abs")
        s_e = sem("softplus_exp")
        s_l = sem("softplus_log")
        s_dt = sem("dt_ready")
        s_xdt = sem("xdt_ready")
        s_dts = sem("dtx_stored")
        s_rep = [sem(f"dtx_spread{j}") for j in range(2)]
        s_dec = sem("decay_ready")
        s_dbu = sem("input_term_ready")
        s_scan = sem("states_ready")
        s_hc = sem("weighted_states_ready")
        s_y = sem("y_unit_summed")
        s_z = sem("in_proj_z")
        s_zc = sem("z_clamped")
        s_sgz = sem("sigmoid_z_part")
        s_sigz = sem("sigmoid_z")
        s_w = sem("silu_z")
        s_yd = sem("y_with_skip")
        s_yz = sem("gated_y_ready")
        s_gl = sem("gate_loaded")
        s_xrl = sem("x_res_loaded")
        s_oc = sem("out_proj_chunk")
        s_og = sem("gated_out")
        s_res = sem("result_ready")
        s_out = sem("result_stored")

        def need(eng, s, v):
            if not (isinstance(v, int) and v <= 0):
                eng.wait_ge(s, v)

        def later(g, par, c, k):
            return g + (c + k) // NC, par ^ ((c + k) // NC & 1), (c + k) % NC

        def exists(g):
            return not isinstance(g, int) or 0 <= g < G

        def item(g, par, c, k, operation, *more):
            gk, park, ck = later(g, par, c, k)
            if exists(gk):
                operation(gk, park, ck, *more)

        def over_groups(eng, step):
            for g in (-2, -1, 0, 1):
                for c in range(NC):
                    step(g, g % 2, c)
            with eng.Fori(1, G // 2 - 1) as i:
                for half in (0, 1):
                    for c in range(NC):
                        step(2 * i + half, half, c)
            for g in (G - 2, G - 1, G):
                for c in range(NC):
                    step(g, g % 2, c)

        block = ctx.enter_context(nc.Block())

        @block.sync
        def _(eng):
            def load_x(g):
                need(eng, s_tr, KD * g)
                eng.dma_start(x_ln[:, :, :], x_g[g]).then_inc(s_xl, 16)

            def store_bc(g, par):
                need(eng, s_xd, g + 1)
                eng.dma_start(bc_dram[par], xdbl[R:RB, :]).then_inc(s_bcst, 16)

            def spread(dst, par, first, k, done):
                rows = bc_dram[par, first:first + N, :].rearrange("(q n) t -> q n t", q=Q)[:, k * HN:(k + 1) * HN, :]
                rows = rows.rearrange("q n t -> q (n t)")[:, None, :].to_broadcast([Q, CB, HN * T])
                eng.dma_start(dst[:, k * HN:(k + 1) * HN, :].rearrange("p n t -> p (n t)"), rows).then_inc(done, 16)

            def load_b(g, par, k):
                if isinstance(g, int) and g == 0:
                    eng.wait_ge(s_bcst, 16)
                need(eng, s_dbu, 2 * (NC * g - 1) + k + 1)
                spread(b_bc, par, 0, k, s_bl[k])

            def load_c(g, par, k):
                need(eng, s_hc, 2 * (NC * g - 1) + k + 1)
                spread(c_bc, par, N, k, s_cl[k])

            def load_out_operands(g):
                need(eng, s_out, 16 * g)
                eng.dma_start(x_res[:, :, :], x_g[g]).then_inc(s_xrl, 16)
                rows = gate_g[g][None, :]
                eng.dma_start(gate[:, :, :].rearrange("p b d -> p (b d)"),
                              rows.to_broadcast([P, BG * D])).then_inc(s_gl, 16)

            def store_out(g):
                need(eng, s_res, BG * (g + 1))
                eng.dma_start(out_g[g], x_res[:, :, :]).then_inc(s_out, 16)

            def spread_dtx(g, par, c):
                s = NC * g + c
                need(eng, s_xdt, s + 1)
                eng.dma_start(dtx_dram[c % 2].rearrange("i c w -> c i w"),
                              dtx[:, :, :].rearrange("p w t -> p (w t)")).then_inc(s_dts, 16)
                need(eng, s_dts, 16 * (s + 1))
                need(eng, s_dbu, 2 * s - 2)
                need(eng, s_dec, 2 * s - 2)
                rows = dtx_dram[c % 2].rearrange("i c w -> i (c w)")[None].to_broadcast([Q, CB, NB * 2 * T])
                eng.dma_start(rep[:, c % 2, :, :, :].rearrange("p c w t -> p (c w t)"),
                              rows).then_inc(s_rep[c % 2], 16)

            gate_g = gate_dram.rearrange("(g b) d -> g (b d)", b=BG)

            eng.dma_start(cond, c_t.rearrange("k p b -> p k b")).then_inc(s_cond, 16)
            load_x(0)
            small = [(ident[:, :], eye), (a_neg[:, :, :], a_log), (cw[:, :, :], conv_w), (cb[:, :], conv_b),
                     (dpar[:, :], d_param), (lng[:, :], ln_g), (lnb[:, :], ln_b), (fold[:, :], eye_blocks),
                     (adb[:, :], ada_b_col), (w_x[:, :, :], xproj_wt.rearrange("k p r -> p k r"))]
            assert len(small) == SMALL
            for dst, src in small:
                eng.dma_start(dst, src).then_inc(s_small, 16)
            eng.dma_start(gate_bias, ada_b_gate.to_broadcast([B, D])).then_inc(s_gb, 16)
            eng.wait_ge(s_wdt, 1)
            eng.dma_start(w_dt[0:R, :], dt_wt).then_inc(s_dtb, 16)
            eng.dma_start(w_dt[RB:RB + 1, :], dt_b).then_inc(s_dtb, 16)
            for k in range(KC):
                eng.dma_start(ada_w[k], ada_wt[k]).then_inc(s_ada, 16)
            eng.dma_start(w_in[:, :, :], in_wt.rearrange("(k p) e -> p k e", p=P)).then_inc(s_win, 16)
            eng.dma_start(w_out[:, :, :], out_wt.rearrange("(k p) e -> p k e", p=P)).then_inc(s_wout, 16)
            eng.wait_ge(s_gate_row, 1)
            eng.dma_start(gate_dram, gate_rows).then_inc(s_gate_st, 16)
            eng.wait_ge(s_gate_st, 16)
            eng.wait_ge(s_mod, 2)

            def step(g, par, c):
                item(g, par, c, 2, spread_dtx)
                if c == 0 and exists(g + 2) and not (isinstance(g, int) and g == -2):
                    load_x(g + 2)
                if c == 3 and exists(g - 1):
                    store_out(g - 1)
                if c == 5 and exists(g + 1):
                    store_bc(g + 1, 1 - par)
                if c == 6 and exists(g + 1):
                    load_b(g + 1, 1 - par, 0)
                if c == 7 and exists(g + 1):
                    load_b(g + 1, 1 - par, 1)
                    load_c(g + 1, 1 - par, 0)
                    load_c(g + 1, 1 - par, 1)
                if c == 7 and exists(g):
                    load_out_operands(g)

            over_groups(eng, step)
            eng.wait_ge(s_out, 16 * G)

        @block.tensor
        def _(pe):
            def transposes(g, half):
                if half == 0:
                    need(pe, s_xhat, BG * (g + 1))
                    need(pe, s_xs, NC * g)
                    need(pe, s_xd, g - 1)
                else:
                    need(pe, s_xn, KD * BG * g + 2 * BG)
                for k in (0, 1):
                    for b in range(BG):
                        last = nc.tensor.transpose(ps_in[:, k * T + b * S:k * T + (b + 1) * S],
                                                   x_ln[:, b, (2 * half + k) * P:(2 * half + k + 1) * P], ident[:, :])
                last.then_inc(s_tr, 2)

            def in_proj_x(g, par, e):
                f = NC * g + e
                if e == 0:
                    need(pe, s_xn, BG * KD * (g + 1))
                need(pe, s_xs, f)
                if e == 2:
                    need(pe, s_xd, g)
                for k in range(KD):
                    last = nc.tensor.matmul(ps_in[:, 0:T], w_in[:, k, e * P:(e + 1) * P], xn[:, k, :],
                                            start=(k == 0), stop=(k == KD - 1))
                last.then_inc(s_xin, 1)

            def convolve(g, par, e):
                f = NC * g + e
                need(pe, s_xs, f + 1)
                need(pe, s_uc, f)
                for j in range(TAPS):
                    last = nc.tensor.matmul(ps_cv[:, 0:T].rearrange("p (b t) -> p b t", b=BG), taps[:, e, j, :],
                                            xs[:, :, j:j + S], start=(j == 0), stop=(j == TAPS - 1))
                last.then_inc(s_cv, 1)

            def x_proj(g, par):
                need(pe, s_u, NC * (g + 1))
                need(pe, s_xs, NC * g + 10 if not isinstance(g, int) else min(NC * g + 10, NC * G))
                for e in range(NC):
                    last = nc.tensor.matmul(ps_in[0:RB, 0:T], w_x[:, e, :], u[:, par, e, :],
                                            start=(e == 0), stop=(e == NC - 1))
                last.then_inc(s_xp, 1)

            def dt_proj(g, par, c):
                s = NC * g + c
                if c == 0:
                    need(pe, s_xd, g + 1)
                need(pe, s_dt, s)
                nc.tensor.matmul(ps_dt, w_dt[:, c * P:(c + 1) * P], xdbl[:, :],
                                 start=True, stop=True).then_inc(s_dtp, 1)

            def in_proj_z(g, par, c):
                if c == 0:
                    need(pe, s_xz, g + 1)
                need(pe, s_zc, NC * g + c)
                for k in range(KD):
                    last = nc.tensor.matmul(ps_z, w_in[:, k, DI + c * P:DI + (c + 1) * P], xz[:, par, k, :],
                                            start=(k == 0), stop=(k == KD - 1))
                last.then_inc(s_z, 1)

            def sum_states(g, par, c, k):
                need(pe, s_hc, 2 * (NC * g + c) + k + 1)
                if k == 0:
                    need(pe, s_yd, NC * g + c - 1)
                for n in range(HN):
                    for j in range(NB):
                        last = nc.tensor.matmul(ps_y[c % 2][j * CB:(j + 1) * CB, 0:T], fold[:, :],
                                                h[:, (2 * c + k) % NH, j, n, :],
                                                start=(k == 0 and n == 0), stop=(k == 1 and n == HN - 1))
                last.then_inc(s_y, 1)

            def out_proj(g, par, c):
                need(pe, s_yz, NC * g + c + 1)
                if c == 0:
                    need(pe, s_og, BG * g)
                if isinstance(g, int) and g == 0 and c == 0:
                    pe.wait_ge(s_wout, 16)
                    pe.wait_ge(s_gate_row, 1)
                for b in range(BG):
                    last = nc.tensor.matmul(ps_o[b][:, 0:D], yz[:, c % 2, b * S:(b + 1) * S], w_out[:, c, :],
                                            start=(c == 0), stop=(c == NC - 1))
                last.then_inc(s_oc, 1)

            pe.wait_ge(s_csilu, 1)
            pe.wait_ge(s_ada, 16 * KC)
            for m in range(2 * KD):
                for k in range(KC):
                    last = nc.tensor.matmul(ps_in[:, m * B:(m + 1) * B], ada_w[k][:, m * P:(m + 1) * P],
                                            cond_s[:, k * B:(k + 1) * B], start=(k == 0), stop=(k == KC - 1))
            last.then_inc(s_ada_mm, 1)
            for k in range(KC):
                last = nc.tensor.matmul(ps_o[0][0:B, 0:D], cond_s[:, k * B:(k + 1) * B],
                                        ada_w[k][:, 2 * D:3 * D], start=(k == 0), stop=(k == KC - 1))
            last.then_inc(s_ada_mm, 1)
            pe.wait_ge(s_small, 16 * SMALL)
            pe.wait_ge(s_mod, 2)
            pe.wait_ge(s_win, 16)
            pe.wait_ge(s_taps, 1)
            pe.wait_ge(s_dtb, 32)
            pe.wait_ge(s_padded, 1)

            def step(g, par, c):
                item(g, par, c, 0, sum_states, 0)
                if c == 2 and exists(g + 2):
                    transposes(g + 2, 0)
                item(g, par, c, 4, dt_proj)
                item(g, par, c, 13, convolve)
                if c == 2 and exists(g + 2):
                    transposes(g + 2, 1)
                item(g, par, c, 14, in_proj_x)
                item(g, par, c, 2, in_proj_z)
                item(g, par, c, -2, out_proj)
                item(g, par, c, 0, sum_states, 1)
                if c == 3 and exists(g + 1):
                    x_proj(g + 1, 1 - par)

            over_groups(pe, step)

        @block.scalar
        def _(act):
            def sigmoid(src, dst, part, done, count):
                nc.scalar.activation(dst, src, ACT.Exp, scale=-1.0).then_inc(part, 1)
                need(act, part, 2 * count + 1)
                nc.scalar.activation(dst, dst, ACT.Ln, bias=1.0).then_inc(part, 1)
                need(act, part, 2 * count + 2)
                nc.scalar.activation(dst, dst, ACT.Exp, scale=-1.0).then_inc(done, 1)

            def rstd_of(g):
                need(act, s_var, g + 1)
                nc.scalar.activation(rstd[:, :], mv[:, :, 1], ACT.Ln, bias=eps_t[:, 0:1]).then_inc(s_lnv, 1)
                need(act, s_lnv, g + 1)
                nc.scalar.activation(rstd[:, :], rstd[:, :], ACT.Exp, scale=-0.5).then_inc(s_rstd, 1)

            def modulate(g, half):
                need(act, s_xin, NC * g)
                need(act, s_xz, g)
                need(act, s_tr, KD * g + 2 * half + 2)
                for k in (0, 1):
                    for b in range(BG):
                        nc.scalar.activation(
                            xn[:, 2 * half + k, b * S:(b + 1) * S],
                            ps_in[:, k * T + b * S:k * T + (b + 1) * S], ACT.Identity,
                            scale=mod_col(mod_a, 2 * half + k, g, b),
                            bias=mod_col(mod_b, 2 * half + k, g, b)).then_inc(s_xn, 1)

            def mod_col(mod, k, g, b):
                return mod[:, k, bass.ds(g * BG + b, 1)]

            def keep_for_z(g, par):
                need(act, s_xn, BG * KD * (g + 1))
                need(act, s_z, NC * (g - 1))
                nc.scalar.activation(xz[:, par, :, :], xn[:, :, :], ACT.Copy).then_inc(s_xz, 1)

            def conv_input(g, par, e):
                f = NC * g + e
                need(act, s_xin, f + 1)
                need(act, s_cv, f)
                nc.scalar.activation(xs[:, :, HALO:HALO + S], ps_in[:, 0:T].rearrange("p (b t) -> p b t", b=BG),
                                     ACT.Copy).then_inc(s_xs, 1)

            def sigmoid_u(g, par, e):
                need(act, s_uc, NC * g + e + 1)
                need(act, s_u, NC * g + e)
                sigmoid(acc[:, :], sig_u[:, :], s_sgu, s_sigu, NC * g + e)

            def xdbl_out(g):
                need(act, s_xp, g + 1)
                need(act, s_bcst, 16 * g)
                need(act, s_dtp, NC * g)
                nc.scalar.activation(xdbl[0:RB, :], ps_in[0:RB, 0:T], ACT.Copy).then_inc(s_xd, 1)

            def softplus(g, par, c):
                s = NC * g + c
                need(act, s_dtp, s + 1)
                need(act, s_dt, s)
                nc.scalar.activation(sp[:, :], ps_dt, ACT.Abs).then_inc(s_abs, 1)
                need(act, s_abs, s + 1)
                nc.scalar.activation(sp[:, :], sp[:, :], ACT.Exp, scale=-1.0).then_inc(s_e, 1)
                need(act, s_e, s + 1)
                nc.scalar.activation(sp[:, :], sp[:, :], ACT.Ln, bias=1.0).then_inc(s_l, 1)

            def decays(g, par, c, k):
                s = NC * g + c
                need(act, s_rep[c % 2], 16 * (NC // 2 * g + c // 2 + 1))
                if isinstance(g, int) and g == 0 and c == 0:
                    act.wait_ge(s_zeroed, 1)
                need(act, s_scan, 2 * s + k - 1)
                for j in range(NB):
                    for n in range(HN):
                        last = nc.scalar.activation(
                            dec[:, k, j, n, :, 1:S],
                            rep[:, c % 2, j, 0, :].rearrange("p (b t) -> p b t", b=BG)[:, :, 1:S],
                            ACT.Exp, scale=a_neg[:, c, j, k * HN + n:k * HN + n + 1])
                last.then_inc(s_dec, 1)

            def sigmoid_of_z(g, par, c):
                s = NC * g + c
                need(act, s_zc, s + 1)
                need(act, s_yz, s - 1)
                sigmoid(z_c[:, c % 2, :], sig_z[:, c % 2, :], s_sgz, s_sigz, s)

            nc.scalar.preload_act_table_set("natural_log_exp_and_others")
            act.wait_ge(s_cmin, 1)
            sigmoid(cond, cond_s, s_csig, s_csig, 0)
            act.wait_ge(s_small, 16 * SMALL)
            nc.scalar.activation(a_neg[:, :, :], a_neg[:, :, :], ACT.Exp).then_inc(s_aexp, 1)
            act.wait_ge(s_aexp, 1)
            nc.scalar.activation(a_neg[:, :, :], a_neg[:, :, :], ACT.Copy, scale=-1.0).then_inc(s_aneg, 1)
            act.wait_ge(s_eps, 1)
            for e in range(NC):
                for j in range(TAPS):
                    last = nc.scalar.activation(taps[:, e, j, :], ident[:, :], ACT.Copy, scale=cw[:, e, j:j + 1])
            last.then_inc(s_taps, 1)
            act.wait_ge(s_mod, 2)
            act.wait_ge(s_padded, 1)
            act.wait_ge(s_aneg, 1)

            def step(g, par, c):
                item(g, par, c, 3, softplus)
                if c == 2 and exists(g + 2):
                    rstd_of(g + 2)
                item(g, par, c, 1, decays, 0)
                item(g, par, c, 13, conv_input)
                item(g, par, c, 1, decays, 1)
                if c == 0 and exists(g + 1):
                    keep_for_z(g + 1, 1 - par)
                if c == 2 and exists(g + 2):
                    modulate(g + 2, 0)
                item(g, par, c, 12, sigmoid_u)
                if c == 4 and exists(g + 1):
                    xdbl_out(g + 1)
                if c == 2 and exists(g + 2):
                    modulate(g + 2, 1)
                item(g, par, c, 0, sigmoid_of_z)

            over_groups(act, step)

        @block.vector
        def _(dve):
            v = nc.vector

            def statistics(g):
                need(dve, s_xl, 16 * (g + 1))
                for b in range(BG):
                    last = v.bn_stats(st6[:, b, :], x_ln[:, b, :])
                last.then_inc(s_st, 1)

            def aggregate():
                for b in range(BG):
                    last = v.bn_aggr(mv[:, b, :], st6[:, b, :])
                last.then_inc(s_var, 1)

            def normalize(g):
                need(dve, s_var, g + 1)
                need(dve, s_rstd, g + 1)
                for b in range(BG):
                    v.tensor_scalar(x_ln[:, b, :], x_ln[:, b, :], mv[:, b, 0:1], rstd[:, b:b + 1],
                                    ALU.subtract, ALU.mult).then_inc(s_xhat, 1)

            def clamp_u(g, par, e):
                f = NC * g + e
                need(dve, s_cv, f + 1)
                need(dve, s_u, f)
                v.tensor_scalar(acc[:, :], ps_cv[:, 0:T], cb[:, e:e + 1], SILU_LOW, ALU.add, ALU.max).then_inc(s_uc, 1)

            def make_dt(g, par, c):
                s = NC * g + c
                need(dve, s_dts, 16 * s)
                need(dve, s_l, s + 1)
                v.scalar_tensor_tensor(out=dtx[:, 0, :], in0=ps_dt, scalar=0.0, in1=sp[:, :],
                                       op0=ALU.max, op1=ALU.add).then_inc(s_dt, 1)

            def make_xdt(g, par, c):
                s = NC * g + c
                need(dve, s_u, s + 1)
                need(dve, s_dt, s + 1)
                v.tensor_tensor(dtx[:, 1, :], dtx[:, 0, :], u[:, par, c, :], ALU.mult).then_inc(s_xdt, 1)

            def input_terms(g, par, c, k):
                s = NC * g + c
                unit = 2 * s + k
                if c == 7 and k == 0 and exists(g + 1):
                    need(dve, s_bcst, 16 * (g + 2))
                if k == 0:
                    need(dve, s_rep[c % 2], 16 * (NC // 2 * g + c // 2 + 1))
                if c == 0:
                    need(dve, s_bl[k], 16 * (g + 1))
                need(dve, s_y, unit - NH + 1)
                v.tensor_tensor(h[:, (2 * c + k) % NH, :, :, :],
                                rep[:, c % 2, :, 1, :][:, :, None, :].to_broadcast([P, NB, HN, T]),
                                b_bc[:, k * HN:(k + 1) * HN, :][:, None, :, :].to_broadcast([P, NB, HN, T]),
                                ALU.mult).then_inc(s_dbu, 1)

            def scan_unit(g, par, c, k):
                unit = 2 * (NC * g + c) + k
                hb = h[:, (2 * c + k) % NH, :, :, :].rearrange("p c n t -> p (c n t)")
                need(dve, s_dbu, unit + 1)
                need(dve, s_dec, unit + 1)
                v.tensor_tensor_scan(hb, dec[:, k, :, :, :, :].rearrange("p c n b t -> p (c n b t)"), hb, 0.0,
                                     ALU.mult, ALU.add).then_inc(s_scan, 1)

            def clamp_z(g, par, c):
                s = NC * g + c
                need(dve, s_z, s + 1)
                need(dve, s_w, s - 1)
                v.tensor_scalar(z_c[:, c % 2, :], ps_z, SILU_LOW, None, ALU.max).then_inc(s_zc, 1)

            def skip(g, par, c):
                s = NC * g + c
                need(dve, s_y, 2 * s + 2)
                need(dve, s_oc, s - 1)
                v.scalar_tensor_tensor(out=yz[:, c % 2, :], in0=u[:, par, c, :], scalar=dpar[:, c:c + 1],
                                       in1=ps_y[c % 2][:, 0:T], op0=ALU.mult, op1=ALU.add).then_inc(s_yd, 1)

            def apply_gate(g):
                need(dve, s_gl, 16 * (g + 1))
                need(dve, s_oc, NC * (g + 1))
                for b in range(BG):
                    v.tensor_tensor(gate[:, b, :], gate[:, b, :], ps_o[b][:, 0:D], ALU.mult).then_inc(s_og, 1)

            v.memset(eps_t[:, :], EPS).then_inc(s_eps, 1)
            dve.wait_ge(s_cond, 16)
            v.tensor_scalar(cond, cond, SILU_LOW, None, ALU.max).then_inc(s_cmin, 1)
            v.memset(w_dt[R:P, :], 0.0).then_inc(s_wdt, 1)
            v.memset(xs[:, :, 0:HALO], 0.0)
            v.memset(xdbl[RB:P, :], 1.0).then_inc(s_padded, 1)
            dve.wait_ge(s_csig, 3)
            dve.wait_ge(s_cmin, 1)
            v.tensor_tensor(cond_s, cond_s, cond, ALU.mult).then_inc(s_csilu, 1)
            dve.wait_ge(s_small, 16 * SMALL)
            v.tensor_scalar(adb[:, KD:2 * KD], adb[:, KD:2 * KD], 1.0, None, ALU.add).then_inc(s_adb1, 1)
            dve.wait_ge(s_ada_mm, 1)
            dve.wait_ge(s_adb1, 1)
            for k in range(KD):
                scale = ps_in[:, (KD + k) * B:(KD + k + 1) * B]
                v.tensor_scalar(mod_t[:, k, :], scale, adb[:, KD + k:KD + k + 1], lnb[:, k:k + 1],
                                ALU.add, ALU.mult).then_inc(s_modt, 1)
                last = v.tensor_scalar(mod_a[:, k, :], scale, adb[:, KD + k:KD + k + 1], lng[:, k:k + 1],
                                       ALU.add, ALU.mult)
            last.then_inc(s_mod, 1)
            dve.wait_ge(s_modt, KD)
            for k in range(KD):
                last = v.scalar_tensor_tensor(out=mod_b[:, k, :], in0=ps_in[:, k * B:(k + 1) * B],
                                              scalar=adb[:, k:k + 1], in1=mod_t[:, k, :], op0=ALU.add, op1=ALU.add)
            last.then_inc(s_mod, 1)
            dve.wait_ge(s_ada_mm, 2)
            dve.wait_ge(s_gb, 16)
            v.tensor_tensor(gate_rows, gate_bias, ps_o[0][0:B, 0:D], ALU.add).then_inc(s_gate_row, 1)

            def step(g, par, c):
                item(g, par, c, 0, input_terms, 0)
                if c == 2 and exists(g + 2):
                    statistics(g + 2)
                if c == 3 and exists(g + 2):
                    normalize(g + 2)
                item(g, par, c, 11, clamp_u)
                item(g, par, c, 2, make_dt)
                item(g, par, c, 0, clamp_z)
                item(g, par, c, 0, scan_unit, 0)
                item(g, par, c, 2, make_xdt)
                item(g, par, c, 0, input_terms, 1)
                if c == 3 and exists(g - 1):
                    apply_gate(g - 1)
                if c == 2 and exists(g + 2):
                    need(dve, s_st, g + 3)
                item(g, par, c, -2, skip)
                if c == 2 and exists(g + 2):
                    aggregate()
                item(g, par, c, 0, scan_unit, 1)

            over_groups(dve, step)

        @block.gpsimd
        def _(pool):
            def weight_states(g, par, c, k):
                unit = 2 * (NC * g + c) + k
                hb = h[:, (2 * c + k) % NH, :, :, :]
                if c == 0:
                    need(pool, s_cl[k], 16 * (g + 1))
                need(pool, s_scan, unit + 1)
                nc.gpsimd.tensor_tensor(hb, hb, c_bc[:, k * HN:(k + 1) * HN, :][:, None, :, :]
                                        .to_broadcast([P, NB, HN, T]), ALU.mult).then_inc(s_hc, 1)

            def make_u(g, par, e):
                need(pool, s_sigu, NC * g + e + 1)
                need(pool, s_yd, NC * (g - 2) + e + 1)
                nc.gpsimd.tensor_tensor(u[:, par, e, :], acc[:, :], sig_u[:, :], ALU.mult).then_inc(s_u, 1)

            def silu_z(g, par, c):
                need(pool, s_sigz, NC * g + c + 1)
                nc.gpsimd.tensor_tensor(sig_z[:, c % 2, :], sig_z[:, c % 2, :], z_c[:, c % 2, :],
                                        ALU.mult).then_inc(s_w, 1)

            def gate_y(g, par, c):
                s = NC * g + c
                need(pool, s_w, s + 1)
                need(pool, s_yd, s + 1)
                nc.gpsimd.tensor_tensor(yz[:, c % 2, :], yz[:, c % 2, :], sig_z[:, c % 2, :],
                                        ALU.mult).then_inc(s_yz, 1)

            def add_residual(g):
                need(pool, s_xrl, 16 * (g + 1))
                for b in range(BG):
                    need(pool, s_og, BG * g + b + 1)
                    nc.gpsimd.tensor_tensor(x_res[:, b, :], x_res[:, b, :], gate[:, b, :],
                                            ALU.add).then_inc(s_res, 1)

            pool.wait_ge(s_ada_mm, 2)
            nc.gpsimd.memset(dec[:, :, :, :, :, :].rearrange("p a c n b t -> p (a c n b t)"), 0.0).then_inc(s_zeroed, 1)

            def step(g, par, c):
                item(g, par, c, 0, weight_states, 0)
                if c == 3 and exists(g - 1):
                    add_residual(g - 1)
                item(g, par, c, 11, make_u)
                item(g, par, c, -1, silu_z)
                item(g, par, c, 0, weight_states, 1)
                item(g, par, c, -2, gate_y)

            over_groups(pool, step)


SMALL = 10


def columns(vector, parts):
    return vector.reshape(parts, P).T


def kernel(x, cond_2048, L0_cond_ln_g, L0_cond_ln_b, L0_cond_ada_w, L0_cond_ada_b, L0_cond_in_proj_w, L0_cond_conv_w,
           L0_cond_conv_b, L0_cond_x_proj_w, L0_cond_dt_proj_w, L0_cond_dt_proj_b, L0_cond_A_log, L0_cond_D_param,
           L0_cond_out_proj_w):
    import numpy as np
    import concourse.bacc as bacc
    from concourse.bass_utils import run_bass_kernel_spmd

    (x, cond, ln_g, ln_b, ada_w, ada_b, in_w, conv_w, conv_b, x_w, dt_w, dt_b, a_log, d_param, out_w) = [
        np.asarray(a) for a in
        (x, cond_2048, L0_cond_ln_g, L0_cond_ln_b, L0_cond_ada_w, L0_cond_ada_b, L0_cond_in_proj_w, L0_cond_conv_w,
         L0_cond_conv_b, L0_cond_x_proj_w, L0_cond_dt_proj_w, L0_cond_dt_proj_b, L0_cond_A_log, L0_cond_D_param,
         L0_cond_out_proj_w)]
    D, DI = x.shape[2], in_w.shape[0] // 2
    kd, nch, kc = D // P, DI // P, cond.shape[1] // P
    arrays = {
        "x": x,
        "c_t": cond.T.reshape(kc, P, cond.shape[0]),
        "ln_g": columns(ln_g, kd),
        "ln_b": columns(ln_b, kd),
        "ada_wt": ada_w.T.reshape(kc, P, 3 * D),
        "ada_b_col": columns(ada_b[0:2 * D], 2 * kd),
        "ada_b_gate": ada_b[2 * D:].reshape(1, D),
        "in_wt": in_w.T,
        "conv_w": conv_w.reshape(nch, P, -1).transpose(1, 0, 2),
        "conv_b": columns(conv_b, nch),
        "xproj_wt": x_w.T.reshape(nch, P, -1),
        "dt_wt": dt_w.T,
        "dt_b": dt_b.reshape(1, DI),
        "a_log": a_log.reshape(nch, 4, 32, 4, 4).transpose(3, 2, 0, 1, 4).reshape(P, nch, 4, 4),
        "d_param": columns(d_param, nch),
        "out_wt": out_w.T,
        "eye": np.eye(P, dtype=np.float32),
        "eye_blocks": np.tile(np.eye(32, dtype=np.float32), (4, 1)),
    }
    arrays = {name: np.ascontiguousarray(a) for name, a in arrays.items()}
    nc = bacc.Bacc("TRN2", target_bir_lowering=False, num_devices=1)
    args = [nc.dram_tensor(name, a.shape, mybir.dt.from_np(a.dtype), kind="ExternalInput").ap()
            for name, a in arrays.items()]
    out = nc.dram_tensor("out", x.shape, mybir.dt.float32, kind="ExternalOutput").ap()
    mamba_block(nc, *args, out)
    got = run_bass_kernel_spmd(nc, [arrays], core_ids=[0])
    return got.results[0]["out"]
```

```python
from contextlib import ExitStack

import concourse.bass as bass
from concourse import mybir

P = 128
Q = 4
CB = P // Q


def mamba_block(nc, x, c_t, ln_g, ln_b, ada_wt, ada_b_col, ada_b_gate, in_wt, conv_w, conv_b, xproj_wt, dt_wt,
                dt_b, a_log, d_param, out_wt, eye, eye_blocks, out):
    F32 = mybir.dt.float32
    ACT = mybir.ActivationFunctionType
    ALU = mybir.AluOpType

    B, S, D = x.shape
    DI = in_wt.shape[1] // 2
    RB = xproj_wt.shape[2]
    R = dt_wt.shape[0]
    N = (RB - R) // 2
    TAPS = conv_w.shape[2]
    KC = c_t.shape[0]
    BG = 2
    G = B // BG
    T = BG * S
    KD = D // P
    NC = DI // P
    NB = P // CB
    QN = N // Q
    HN = QN // 2
    U = NB * HN * T
    NH = 4
    HALO = TAPS - 1
    EPS = 1e-5
    SILU_LOW = -40.0

    bc_dram = nc.dram_tensor("bc_rows", (2, 2 * N, T), F32, kind="Internal").ap()
    dtx_dram = nc.dram_tensor("dtx_rows", (2, CB, NB, 2 * T), F32, kind="Internal").ap()
    gate_dram = nc.dram_tensor("gate_rows", (B, D), F32, kind="Internal").ap()
    x_g = x.rearrange("(g b) t d -> g t b d", b=BG)
    out_g = out.rearrange("(g b) t d -> g t b d", b=BG)

    ctx = ExitStack()
    with ctx:
        def sb(name, shape):
            return ctx.enter_context(nc.sbuf_tensor(name, shape, F32))

        def sem(name):
            return ctx.enter_context(nc.semaphore(name))

        w_in = sb("w_in", [P, KD, 2 * DI])
        w_out = sb("w_out", [P, NC, D])
        w_x = sb("w_x", [P, NC, RB])
        w_dt = sb("w_dt", [P, DI])
        a_neg = sb("a_neg", [P, NC, NB, QN])
        cw = sb("cw", [P, NC, TAPS])
        cb = sb("cb", [P, NC])
        dpar = sb("dpar", [P, NC])
        lng = sb("lng", [P, KD])
        lnb = sb("lnb", [P, KD])
        adb = sb("adb", [P, 2 * KD])
        ident = sb("ident", [P, P])
        fold = sb("fold", [P, CB])
        taps = sb("taps", [P, NC, TAPS, P])
        diag_d = sb("diag_d", [P, NC, P])
        eps_t = sb("eps_t", [P, 1])
        mod_a = sb("mod_a", [P, KD, B])
        mod_b = sb("mod_b", [P, KD, B])
        x_ln = sb("x_ln", [P, BG, D])
        st6 = sb("st6", [P, BG, 6])
        mv = sb("mv", [P, BG, 2])
        rstd = sb("rstd", [P, BG])
        xn = sb("xn", [P, KD, T])
        xz = sb("xz", [P, 2, KD, T])
        xs = sb("xs", [P, 2, BG, HALO + S])
        acc = sb("acc", [P, T])
        sig_u = sb("sig_u", [P, T])
        u = sb("u", [P, 2, NC, T])
        xdbl = sb("xdbl", [P, T])
        b_bc = sb("b_bc", [P, QN, T])
        c_bc = sb("c_bc", [P, QN, T])
        sp = sb("sp", [P, T])
        dtx = sb("dtx", [P, 2, T])
        rep = sb("rep", [P, 2, NB, 2, T])
        z_c = sb("z_c", [P, 2, T])
        sig_z = sb("sig_z", [P, 2, T])
        dec = sb("dec", [P, 2, NB, HN, BG, S])
        h = sb("h", [P, NH, NB, HN, T])
        yz = sb("yz", [P, 2, T])
        x_res = sb("x_res", [P, BG, D])
        gate = sb("gate", [P, BG, D])

        pb = [ctx.enter_context(nc.psum_tensor(f"pb{i}", [P, 512], F32)) for i in range(8)]
        ps_in = pb[0]
        ps_cv = pb[1]
        ps_dt = pb[2][:, 0:T]
        ps_z = pb[3][:, 0:T]
        ps_y = pb[4:6]
        ps_o = pb[6:8]
        ps_ada = (pb[2], pb[3], ps_o[0])

        ada_w = [flat[:, j * 3 * D:(j + 1) * 3 * D]
                 for flat in (h[:, :, :, :, :].rearrange("p a c n t -> p (a c n t)"),
                              dec[:, :, :, :, :, :].rearrange("p a c n b t -> p (a c n b t)"),
                              u[:, :, :, :].rearrange("p a c t -> p (a c t)"))
                 for j in range(flat.shape[1] // (3 * D))][0:KC]
        rep_flat = rep[:, :, :, :, :].rearrange("p a c w t -> p (a c w t)")
        used = [0]

        def lend(rows, n):
            used[0] += n
            return rep_flat[0:rows, used[0] - n:used[0]]

        cond, cond_s = lend(P, KC * B), lend(P, KC * B)
        gate_bias, gate_rows = lend(B, D), lend(B, D)
        ada_rows = lend(B, 2 * D)
        mod_t = lend(P, KD * B).rearrange("p (k b) -> p k b", k=KD)

        s_cond = sem("cond_loaded")
        s_small = sem("small_loaded")
        s_ada = [sem(f"ada_loaded{k}") for k in range(KC)]
        s_win = [sem(f"w_in_loaded_{half}") for half in "xz"]
        s_late = sem("later_weights_loaded")
        s_wout = sem("w_out_loaded")
        s_gb = sem("gate_bias_loaded")
        s_wdt = sem("w_dt_zeroed")
        s_padded = sem("constant_parts_ready")
        s_zeroed = sem("zeroed")
        s_taps = sem("taps_ready")
        s_eps = sem("eps_ready")
        s_cmin = sem("cond_clamped")
        s_csig = sem("cond_sigmoid_part")
        s_csilu = sem("cond_silu")
        s_ada_mm = sem("ada_products")
        s_ada_row = sem("ada_rows_ready")
        s_ada_tr = sem("ada_rows_transposed")
        s_gate_row = sem("gate_row_ready")
        s_gate_st = sem("gate_rows_stored")
        s_adb1 = sem("scale_bias_plus_one")
        s_modt = sem("mod_b_part")
        s_mod = sem("mod_ready")
        s_aexp = sem("a_exp")
        s_aneg = sem("a_neg_ready")
        s_xl = sem("x_loaded")
        s_st = sem("stats_taken")
        s_var = sem("var_ready")
        s_lnv = sem("ln_var")
        s_rstd = sem("rstd_ready")
        s_xhat = sem("xhat_ready")
        s_tr = sem("xhat_transposed")
        s_xn = sem("xn_ready")
        s_xz = sem("xz_ready")
        s_xin = sem("in_proj_x")
        s_xs = sem("conv_input_ready")
        s_cv = sem("conv_products")
        s_uc = sem("conv_clamped")
        s_sgu = sem("sigmoid_u_part")
        s_sigu = sem("sigmoid_u")
        s_u = sem("u_ready")
        s_xp = sem("x_proj")
        s_xd = sem("xdbl_ready")
        s_bcst = sem("bc_rows_stored")
        s_bl = [sem(f"b_loaded{k}") for k in range(2)]
        s_cl = [sem(f"c_loaded{k}") for k in range(2)]
        s_dtp = sem("dt_proj")
        s_abs = sem("softplus_abs")
        s_e = sem("softplus_exp")
        s_l = sem("softplus_log")
        s_dt = sem("dt_ready")
        s_xdt = sem("xdt_ready")
        s_dts = sem("dtx_stored")
        s_rep = [sem(f"dtx_spread{j}") for j in range(2)]
        s_dec = sem("decay_ready")
        s_dbu = sem("input_term_ready")
        s_scan = sem("states_ready")
        s_hc = sem("weighted_states_ready")
        s_y = sem("y_unit_summed")
        s_z = sem("in_proj_z")
        s_zc = sem("z_clamped")
        s_sgz = sem("sigmoid_z_part")
        s_sigz = sem("sigmoid_z")
        s_w = sem("silu_z")
        s_skip = sem("skip_product")
        s_yz = sem("gated_y_ready")
        s_gl = sem("gate_loaded")
        s_xrl = sem("x_res_loaded")
        s_oc = sem("out_proj_chunk")
        s_og = sem("gated_out")
        s_res = sem("result_ready")
        s_out = sem("result_stored")

        def need(eng, s, v):
            if not (isinstance(v, int) and v <= 0):
                eng.wait_ge(s, v)

        def later(g, par, c, k):
            return g + (c + k) // NC, par ^ ((c + k) // NC & 1), (c + k) % NC

        def exists(g):
            return not isinstance(g, int) or 0 <= g < G

        def pool_makes_xdt(c):
            return c % 4 == 1

        def begins(g):
            return isinstance(g, int) and g == 0

        def item(g, par, c, k, operation, *more):
            gk, park, ck = later(g, par, c, k)
            if exists(gk):
                operation(gk, park, ck, *more)

        def over_groups(eng, step):
            for g in (-2, -1, 0, 1):
                for c in range(NC):
                    step(g, g % 2, c)
            with eng.Fori(1, G // 2 - 1) as i:
                for half in (0, 1):
                    for c in range(NC):
                        step(2 * i + half, half, c)
            for g in (G - 2, G - 1, G):
                for c in range(NC):
                    step(g, g % 2, c)

        block = ctx.enter_context(nc.Block())

        @block.sync
        def _(eng):
            def load_x(g):
                need(eng, s_tr, KD * g)
                eng.dma_start(x_ln[:, :, :], x_g[g]).then_inc(s_xl, 16)

            def store_bc(g, par):
                need(eng, s_xd, g + 1)
                eng.dma_start(bc_dram[par], xdbl[R:RB, :]).then_inc(s_bcst, 16)

            def spread(dst, par, first, k, done):
                rows = bc_dram[par, first:first + N, :].rearrange("(q n) t -> q n t", q=Q)[:, k * HN:(k + 1) * HN, :]
                rows = rows.rearrange("q n t -> q (n t)")[:, None, :].to_broadcast([Q, CB, HN * T])
                eng.dma_start(dst[:, k * HN:(k + 1) * HN, :].rearrange("p n t -> p (n t)"), rows).then_inc(done, 16)

            def load_b(g, par, k):
                if begins(g):
                    eng.wait_ge(s_bcst, 16)
                need(eng, s_dbu, 2 * (NC * g - 1) + k + 1)
                spread(b_bc, par, 0, k, s_bl[k])

            def load_c(g, par, k):
                need(eng, s_hc, 2 * (NC * g - 1) + k + 1)
                spread(c_bc, par, N, k, s_cl[k])

            def load_out_operands(g):
                need(eng, s_out, 16 * g)
                eng.dma_start(x_res[:, :, :], x_g[g]).then_inc(s_xrl, 16)
                rows = gate_g[g][None, :]
                eng.dma_start(gate[:, :, :].rearrange("p b d -> p (b d)"),
                              rows.to_broadcast([P, BG * D])).then_inc(s_gl, 16)

            def store_out(g):
                need(eng, s_res, BG * (g + 1))
                eng.dma_start(out_g[g], x_res[:, :, :]).then_inc(s_out, 16)

            def store_dtx(g, par, c):
                s = NC * g + c
                need(eng, s_xdt, s + 1)
                eng.dma_start(dtx_dram[c % 2].rearrange("i c w -> c i w"),
                              dtx[:, :, :].rearrange("p w t -> p (w t)")).then_inc(s_dts, 16)

            def spread_dtx(g, par, c):
                s = NC * g + c
                need(eng, s_dts, 16 * (s + 1))
                need(eng, s_dbu, 2 * s - 2)
                need(eng, s_dec, 2 * s - 2)
                rows = dtx_dram[c % 2].rearrange("i c w -> i (c w)")[None].to_broadcast([Q, CB, NB * 2 * T])
                eng.dma_start(rep[:, c % 2, :, :, :].rearrange("p c w t -> p (c w t)"),
                              rows).then_inc(s_rep[c % 2], 16)

            gate_g = gate_dram.rearrange("(g b) d -> g (b d)", b=BG)

            eng.dma_start(cond, c_t.rearrange("k p b -> p k b")).then_inc(s_cond, 16)
            load_x(0)
            small = [(ident[:, :], eye), (a_neg[:, :, :], a_log), (cw[:, :, :], conv_w), (cb[:, :], conv_b),
                     (dpar[:, :], d_param), (lng[:, :], ln_g), (lnb[:, :], ln_b), (adb[:, :], ada_b_col)]
            assert len(small) == SMALL
            for dst, src in small:
                eng.dma_start(dst, src).then_inc(s_small, 16)
            for k in range(KC):
                eng.dma_start(ada_w[k], ada_wt[k]).then_inc(s_ada[k], 16)
            in_rows = in_wt.rearrange("(k p) e -> p k e", p=P)
            eng.dma_start(w_in[:, :, 0:DI], in_rows[:, :, 0:DI]).then_inc(s_win[0], 16)
            eng.dma_start(gate_bias, ada_b_gate.to_broadcast([B, D])).then_inc(s_gb, 16)
            eng.dma_start(fold[:, :], eye_blocks).then_inc(s_late, 16)
            eng.dma_start(w_x[:, :, :], xproj_wt.rearrange("k p r -> p k r")).then_inc(s_late, 16)
            eng.wait_ge(s_wdt, 1)
            eng.dma_start(w_dt[0:R, :], dt_wt).then_inc(s_late, 16)
            eng.dma_start(w_dt[RB:RB + 1, :], dt_b).then_inc(s_late, 16)
            eng.dma_start(w_in[:, :, DI:2 * DI], in_rows[:, :, DI:2 * DI]).then_inc(s_win[1], 16)
            eng.dma_start(w_out[:, :, :], out_wt.rearrange("(k p) e -> p k e", p=P)).then_inc(s_wout, 16)
            eng.wait_ge(s_gate_row, 1)
            eng.dma_start(gate_dram, gate_rows).then_inc(s_gate_st, 16)
            eng.wait_ge(s_gate_st, 16)
            eng.wait_ge(s_mod, 2)

            def step(g, par, c):
                item(g, par, c, 2, spread_dtx)
                if c == 5 and exists(g + 1):
                    store_bc(g + 1, 1 - par)
                item(g, par, c, 3, store_dtx)
                if c == 6 and exists(g + 1):
                    load_b(g + 1, 1 - par, 1)
                if c == 5 and exists(g + 1):
                    load_b(g + 1, 1 - par, 0)
                if c == 7 and exists(g):
                    load_out_operands(g)
                if c == 0 and not begins(g + 2) and exists(g + 2):
                    load_x(g + 2)
                if c == 7 and exists(g + 1):
                    load_c(g + 1, 1 - par, 1)
                if c == 4 and exists(g - 1):
                    store_out(g - 1)
                if c == 6 and exists(g + 1):
                    load_c(g + 1, 1 - par, 0)

            over_groups(eng, step)
            eng.wait_ge(s_out, 16 * G)

        @block.tensor
        def _(pe):
            def transposes(g, half):
                if half == 0:
                    need(pe, s_xhat, BG * (g + 1))
                    need(pe, s_xs, NC * g)
                    need(pe, s_xd, g - 1)
                else:
                    need(pe, s_xn, KD * BG * g + 2 * BG)
                for k in (0, 1):
                    for b in range(BG):
                        last = nc.tensor.transpose(ps_in[:, k * T + b * S:k * T + (b + 1) * S],
                                                   x_ln[:, b, (2 * half + k) * P:(2 * half + k + 1) * P], ident[:, :])
                last.then_inc(s_tr, 2)

            def in_proj_x(g, par, e):
                f = NC * g + e
                if begins(g) and e == 0:
                    pe.wait_ge(s_win[0], 16)
                if e == 0:
                    need(pe, s_xn, BG * KD * (g + 1))
                need(pe, s_xs, f)
                if e == 2:
                    need(pe, s_xd, g)
                for k in range(KD):
                    last = nc.tensor.matmul(ps_in[:, 0:T], w_in[:, k, e * P:(e + 1) * P], xn[:, k, :],
                                            start=(k == 0), stop=(k == KD - 1))
                last.then_inc(s_xin, 1)

            def convolve(g, par, e):
                f = NC * g + e
                if begins(g) and e == 0:
                    pe.wait_ge(s_mod, 2)
                need(pe, s_xs, f + 1)
                need(pe, s_uc, f)
                for j in range(TAPS):
                    last = nc.tensor.matmul(ps_cv[:, 0:T].rearrange("p (b t) -> p b t", b=BG), taps[:, e, j, :],
                                            xs[:, e % 2, :, j:j + S], start=(j == 0), stop=(j == TAPS - 1))
                last.then_inc(s_cv, 1)

            def x_proj(g, par):
                if begins(g):
                    pe.wait_ge(s_late, 64)
                need(pe, s_u, NC * (g + 1))
                ahead = NC * g + 10
                need(pe, s_xs, min(ahead, NC * G) if isinstance(g, int) else ahead)
                for e in range(NC):
                    last = nc.tensor.matmul(ps_in[0:RB, 0:T], w_x[:, e, :], u[:, par, e, :],
                                            start=(e == 0), stop=(e == NC - 1))
                last.then_inc(s_xp, 1)

            def dt_proj(g, par, c):
                s = NC * g + c
                if c == 0:
                    need(pe, s_xd, g + 1)
                need(pe, s_dt, s)
                nc.tensor.matmul(ps_dt, w_dt[:, c * P:(c + 1) * P], xdbl[:, :],
                                 start=True, stop=True).then_inc(s_dtp, 1)

            def in_proj_z(g, par, c):
                if begins(g) and c == 0:
                    pe.wait_ge(s_win[1], 16)
                if c == 0:
                    need(pe, s_xz, g + 1)
                need(pe, s_zc, NC * g + c)
                for k in range(KD):
                    last = nc.tensor.matmul(ps_z, w_in[:, k, DI + c * P:DI + (c + 1) * P], xz[:, par, k, :],
                                            start=(k == 0), stop=(k == KD - 1))
                last.then_inc(s_z, 1)

            def skip(g, par, c):
                need(pe, s_yz, NC * g + c - 1)
                nc.tensor.matmul(ps_y[c % 2][:, 0:T], diag_d[:, c, :], u[:, par, c, :],
                                 start=True, stop=False).then_inc(s_skip, 1)

            def sum_states(g, par, c, k):
                need(pe, s_hc, 2 * (NC * g + c) + k + 1)
                for n in range(HN):
                    for j in range(NB):
                        last = nc.tensor.matmul(ps_y[c % 2][j * CB:(j + 1) * CB, 0:T], fold[:, :],
                                                h[:, (2 * c + k) % NH, j, n, :],
                                                start=False, stop=(k == 1 and n == HN - 1))
                last.then_inc(s_y, 1)

            def out_proj(g, par, c):
                need(pe, s_yz, NC * g + c + 1)
                if c == 0:
                    need(pe, s_og, BG * g)
                if begins(g) and c == 0:
                    pe.wait_ge(s_wout, 16)
                    pe.wait_ge(s_gate_row, 1)
                for b in range(BG):
                    last = nc.tensor.matmul(ps_o[b][:, 0:D], yz[:, c % 2, b * S:(b + 1) * S], w_out[:, c, :],
                                            start=(c == 0), stop=(c == NC - 1))
                last.then_inc(s_oc, 1)

            pe.wait_ge(s_csilu, 1)
            for k in range(KC):
                pe.wait_ge(s_ada[k], 16)
                for part in range(3):
                    last = nc.tensor.matmul(ps_ada[part][0:B, 0:D], cond_s[:, k * B:(k + 1) * B],
                                            ada_w[k][:, part * D:(part + 1) * D], start=(k == 0), stop=(k == KC - 1))
            last.then_inc(s_ada_mm, 1)
            pe.wait_ge(s_small, 16 * SMALL)
            pe.wait_ge(s_ada_row, 2)
            for m in range(2 * KD):
                last = nc.tensor.transpose(ps_cv[:, m * B:(m + 1) * B], ada_rows[:, m * P:(m + 1) * P],
                                           ident[0:B, 0:B])
            last.then_inc(s_ada_tr, 1)
            pe.wait_ge(s_taps, 2)
            pe.wait_ge(s_padded, 1)

            def step(g, par, c):
                item(g, par, c, 0, sum_states, 0)
                item(g, par, c, 4, dt_proj)
                item(g, par, c, 1, skip)
                if c == 2 and exists(g + 2):
                    transposes(g + 2, 1)
                item(g, par, c, 13, convolve)
                item(g, par, c, -2, out_proj)
                item(g, par, c, 14, in_proj_x)
                item(g, par, c, 0, sum_states, 1)
                if c == 1 and exists(g + 2):
                    transposes(g + 2, 0)
                item(g, par, c, 2, in_proj_z)
                if c == 3 and exists(g + 1):
                    x_proj(g + 1, 1 - par)

            over_groups(pe, step)

        @block.scalar
        def _(act):
            def sigmoid(src, dst, part, done, count):
                nc.scalar.activation(dst, src, ACT.Exp, scale=-1.0).then_inc(part, 1)
                need(act, part, 2 * count + 1)
                nc.scalar.activation(dst, dst, ACT.Ln, bias=1.0).then_inc(part, 1)
                need(act, part, 2 * count + 2)
                nc.scalar.activation(dst, dst, ACT.Exp, scale=-1.0).then_inc(done, 1)

            def rstd_of(g):
                need(act, s_var, g + 1)
                nc.scalar.activation(rstd[:, :], mv[:, :, 1], ACT.Ln, bias=eps_t[:, 0:1]).then_inc(s_lnv, 1)
                need(act, s_lnv, g + 1)
                nc.scalar.activation(rstd[:, :], rstd[:, :], ACT.Exp, scale=-0.5).then_inc(s_rstd, 1)

            def modulate(g, half):
                need(act, s_xin, NC * g)
                need(act, s_xz, g)
                need(act, s_tr, KD * g + 2 * half + 2)
                for k in (0, 1):
                    for b in range(BG):
                        nc.scalar.activation(
                            xn[:, 2 * half + k, b * S:(b + 1) * S],
                            ps_in[:, k * T + b * S:k * T + (b + 1) * S], ACT.Identity,
                            scale=mod_col(mod_a, 2 * half + k, g, b),
                            bias=mod_col(mod_b, 2 * half + k, g, b)).then_inc(s_xn, 1)

            def mod_col(mod, k, g, b):
                return mod[:, k, bass.ds(g * BG + b, 1)]

            def keep_for_z(g, par):
                need(act, s_xn, BG * KD * (g + 1))
                need(act, s_z, NC * (g - 1))
                nc.scalar.activation(xz[:, par, :, :], xn[:, :, :], ACT.Copy).then_inc(s_xz, 1)

            def conv_input(g, par, e):
                f = NC * g + e
                need(act, s_xin, f + 1)
                need(act, s_cv, f - 1)
                nc.scalar.activation(xs[:, e % 2, :, HALO:HALO + S], ps_in[:, 0:T].rearrange("p (b t) -> p b t", b=BG),
                                     ACT.Copy).then_inc(s_xs, 1)

            def sigmoid_u(g, par, e):
                need(act, s_uc, NC * g + e + 1)
                need(act, s_u, NC * g + e)
                sigmoid(acc[:, :], sig_u[:, :], s_sgu, s_sigu, NC * g + e)

            def xdbl_out(g):
                need(act, s_xp, g + 1)
                need(act, s_bcst, 16 * g)
                need(act, s_dtp, NC * g)
                nc.scalar.activation(xdbl[0:RB, :], ps_in[0:RB, 0:T], ACT.Copy).then_inc(s_xd, 1)

            def softplus(g, par, c):
                s = NC * g + c
                need(act, s_dtp, s + 1)
                need(act, s_dt, s)
                nc.scalar.activation(sp[:, :], ps_dt, ACT.Abs).then_inc(s_abs, 1)
                need(act, s_abs, s + 1)
                nc.scalar.activation(sp[:, :], sp[:, :], ACT.Exp, scale=-1.0).then_inc(s_e, 1)
                need(act, s_e, s + 1)
                nc.scalar.activation(sp[:, :], sp[:, :], ACT.Ln, bias=1.0).then_inc(s_l, 1)

            def decays(g, par, c, k):
                s = NC * g + c
                need(act, s_rep[c % 2], 16 * (NC // 2 * g + c // 2 + 1))
                if begins(g) and c == 0:
                    act.wait_ge(s_zeroed, 1)
                need(act, s_scan, 2 * s + k - 1)
                for j in range(NB):
                    for n in range(HN):
                        last = nc.scalar.activation(
                            dec[:, k, j, n, :, 1:S],
                            rep[:, c % 2, j, 0, :].rearrange("p (b t) -> p b t", b=BG)[:, :, 1:S],
                            ACT.Exp, scale=a_neg[:, c, j, k * HN + n:k * HN + n + 1])
                last.then_inc(s_dec, 1)

            def sigmoid_of_z(g, par, c):
                s = NC * g + c
                need(act, s_zc, s + 1)
                need(act, s_yz, s - 1)
                sigmoid(z_c[:, c % 2, :], sig_z[:, c % 2, :], s_sgz, s_sigz, s)

            nc.scalar.preload_act_table_set("natural_log_exp_and_others")
            act.wait_ge(s_cmin, 1)
            sigmoid(cond, cond_s, s_csig, s_csig, 0)
            act.wait_ge(s_small, 16 * SMALL)
            nc.scalar.activation(a_neg[:, :, :], a_neg[:, :, :], ACT.Exp).then_inc(s_aexp, 1)
            act.wait_ge(s_aexp, 1)
            nc.scalar.activation(a_neg[:, :, :], a_neg[:, :, :], ACT.Copy, scale=-1.0).then_inc(s_aneg, 1)
            act.wait_ge(s_eps, 1)
            rstd_of(0)
            for e in range(NC):
                for j in range(TAPS):
                    last = nc.scalar.activation(taps[:, e, j, :], ident[:, :], ACT.Copy, scale=cw[:, e, j:j + 1])
            last.then_inc(s_taps, 1)
            for e in range(NC):
                last = nc.scalar.activation(diag_d[:, e, :], ident[:, :], ACT.Copy, scale=dpar[:, e:e + 1])
            last.then_inc(s_taps, 1)
            act.wait_ge(s_ada_mm, 1)
            for part in (0, 1):
                nc.scalar.activation(ada_rows[:, part * D:(part + 1) * D], ps_ada[part][0:B, 0:D],
                                     ACT.Copy).then_inc(s_ada_row, 1)
            act.wait_ge(s_mod, 2)
            act.wait_ge(s_padded, 1)
            act.wait_ge(s_aneg, 1)

            def step(g, par, c):
                item(g, par, c, 1, decays, 0)
                item(g, par, c, 0, sigmoid_of_z)
                item(g, par, c, 13, conv_input)
                if c == 0 and exists(g + 1):
                    keep_for_z(g + 1, 1 - par)
                item(g, par, c, 1, decays, 1)
                if c == 2 and exists(g + 2):
                    modulate(g + 2, 0)
                if c == 4 and exists(g + 1):
                    xdbl_out(g + 1)
                item(g, par, c, 12, sigmoid_u)
                item(g, par, c, 4, softplus)
                if c == 1 and not begins(g + 2) and exists(g + 2):
                    rstd_of(g + 2)
                if c == 2 and exists(g + 2):
                    modulate(g + 2, 1)

            over_groups(act, step)

        @block.vector
        def _(dve):
            v = nc.vector

            def statistics(g):
                need(dve, s_xl, 16 * (g + 1))
                for b in range(BG):
                    last = v.bn_stats(st6[:, b, :], x_ln[:, b, :])
                last.then_inc(s_st, 1)

            def aggregate():
                for b in range(BG):
                    last = v.bn_aggr(mv[:, b, :], st6[:, b, :])
                last.then_inc(s_var, 1)

            def normalize(g):
                need(dve, s_var, g + 1)
                need(dve, s_rstd, g + 1)
                for b in range(BG):
                    v.tensor_scalar(x_ln[:, b, :], x_ln[:, b, :], mv[:, b, 0:1], rstd[:, b:b + 1],
                                    ALU.subtract, ALU.mult).then_inc(s_xhat, 1)

            def clamp_u(g, par, e):
                f = NC * g + e
                need(dve, s_cv, f + 1)
                need(dve, s_u, f)
                v.tensor_scalar(acc[:, :], ps_cv[:, 0:T], cb[:, e:e + 1], SILU_LOW, ALU.add, ALU.max).then_inc(s_uc, 1)

            def make_dt(g, par, c):
                s = NC * g + c
                need(dve, s_dts, 16 * s)
                need(dve, s_l, s + 1)
                v.scalar_tensor_tensor(out=dtx[:, 0, :], in0=ps_dt, scalar=0.0, in1=sp[:, :],
                                       op0=ALU.max, op1=ALU.add).then_inc(s_dt, 1)

            def make_xdt(g, par, c):
                s = NC * g + c
                if pool_makes_xdt(c):
                    return
                need(dve, s_u, s + 1)
                need(dve, s_dt, s + 1)
                v.tensor_tensor(dtx[:, 1, :], dtx[:, 0, :], u[:, par, c, :], ALU.mult).then_inc(s_xdt, 1)

            def input_terms(g, par, c, k):
                s = NC * g + c
                unit = 2 * s + k
                if c == 7 and k == 0 and exists(g + 1):
                    need(dve, s_bcst, 16 * (g + 2))
                if k == 0:
                    need(dve, s_rep[c % 2], 16 * (NC // 2 * g + c // 2 + 1))
                if c == 0:
                    need(dve, s_bl[k], 16 * (g + 1))
                need(dve, s_y, unit - NH + 1)
                v.tensor_tensor(h[:, (2 * c + k) % NH, :, :, :],
                                rep[:, c % 2, :, 1, :][:, :, None, :].to_broadcast([P, NB, HN, T]),
                                b_bc[:, k * HN:(k + 1) * HN, :][:, None, :, :].to_broadcast([P, NB, HN, T]),
                                ALU.mult).then_inc(s_dbu, 1)

            def scan_unit(g, par, c, k):
                unit = 2 * (NC * g + c) + k
                hb = h[:, (2 * c + k) % NH, :, :, :].rearrange("p c n t -> p (c n t)")
                need(dve, s_dbu, unit + 1)
                need(dve, s_dec, unit + 1)
                v.tensor_tensor_scan(hb, dec[:, k, :, :, :, :].rearrange("p c n b t -> p (c n b t)"), hb, 0.0,
                                     ALU.mult, ALU.add).then_inc(s_scan, 1)

            def clamp_z(g, par, c):
                s = NC * g + c
                need(dve, s_z, s + 1)
                need(dve, s_w, s - 1)
                v.tensor_scalar(z_c[:, c % 2, :], ps_z, SILU_LOW, None, ALU.max).then_inc(s_zc, 1)

            def gate_y(g, par, c):
                s = NC * g + c
                need(dve, s_w, s + 1)
                need(dve, s_y, 2 * s + 2)
                need(dve, s_oc, s - 1)
                v.tensor_tensor(yz[:, c % 2, :], ps_y[c % 2][:, 0:T], sig_z[:, c % 2, :],
                                ALU.mult).then_inc(s_yz, 1)

            def apply_gate(g):
                need(dve, s_gl, 16 * (g + 1))
                need(dve, s_oc, NC * (g + 1))
                for b in range(BG):
                    v.tensor_tensor(gate[:, b, :], gate[:, b, :], ps_o[b][:, 0:D], ALU.mult).then_inc(s_og, 1)

            v.memset(eps_t[:, :], EPS).then_inc(s_eps, 1)
            dve.wait_ge(s_cond, 16)
            v.tensor_scalar(cond, cond, SILU_LOW, None, ALU.max).then_inc(s_cmin, 1)
            v.memset(w_dt[R:P, :], 0.0).then_inc(s_wdt, 1)
            for half in (0, 1):
                v.memset(xs[:, half, :, 0:HALO], 0.0)
            v.memset(xdbl[RB:P, :], 1.0).then_inc(s_padded, 1)
            dve.wait_ge(s_csig, 3)
            dve.wait_ge(s_cmin, 1)
            v.tensor_tensor(cond_s, cond_s, cond, ALU.mult).then_inc(s_csilu, 1)
            statistics(0)
            dve.wait_ge(s_st, 1)
            aggregate()
            dve.wait_ge(s_small, 16 * SMALL)
            v.tensor_scalar(adb[:, KD:2 * KD], adb[:, KD:2 * KD], 1.0, None, ALU.add).then_inc(s_adb1, 1)
            normalize(0)
            dve.wait_ge(s_ada_tr, 1)
            dve.wait_ge(s_adb1, 1)
            for k in range(KD):
                scale = ps_cv[:, (KD + k) * B:(KD + k + 1) * B]
                v.tensor_scalar(mod_t[:, k, :], scale, adb[:, KD + k:KD + k + 1], lnb[:, k:k + 1],
                                ALU.add, ALU.mult).then_inc(s_modt, 1)
                last = v.tensor_scalar(mod_a[:, k, :], scale, adb[:, KD + k:KD + k + 1], lng[:, k:k + 1],
                                       ALU.add, ALU.mult)
            last.then_inc(s_mod, 1)
            dve.wait_ge(s_modt, KD)
            for k in range(KD):
                last = v.scalar_tensor_tensor(out=mod_b[:, k, :], in0=ps_cv[:, k * B:(k + 1) * B],
                                              scalar=adb[:, k:k + 1], in1=mod_t[:, k, :], op0=ALU.add, op1=ALU.add)
            last.then_inc(s_mod, 1)
            dve.wait_ge(s_gb, 16)
            v.tensor_tensor(gate_rows, gate_bias, ps_o[0][0:B, 0:D], ALU.add).then_inc(s_gate_row, 1)

            def step(g, par, c):
                item(g, par, c, 0, input_terms, 0)
                if c == 2 and not begins(g + 2) and exists(g + 2):
                    statistics(g + 2)
                item(g, par, c, 11, clamp_u)
                if c == 3 and not begins(g + 2) and exists(g + 2):
                    normalize(g + 2)
                item(g, par, c, 0, scan_unit, 0)
                if c == 2 and not begins(g + 2) and exists(g + 2):
                    need(dve, s_st, g + 3)
                item(g, par, c, -2, gate_y)
                if c == 3 and exists(g - 1):
                    apply_gate(g - 1)
                if c == 2 and not begins(g + 2) and exists(g + 2):
                    aggregate()
                item(g, par, c, 2, make_xdt)
                item(g, par, c, 0, input_terms, 1)
                item(g, par, c, 0, scan_unit, 1)
                item(g, par, c, 0, clamp_z)
                item(g, par, c, 3, make_dt)

            over_groups(dve, step)

        @block.gpsimd
        def _(pool):
            def weight_states(g, par, c, k):
                unit = 2 * (NC * g + c) + k
                hb = h[:, (2 * c + k) % NH, :, :, :]
                if c == 0:
                    need(pool, s_cl[k], 16 * (g + 1))
                need(pool, s_scan, unit + 1)
                nc.gpsimd.tensor_tensor(hb, hb, c_bc[:, k * HN:(k + 1) * HN, :][:, None, :, :]
                                        .to_broadcast([P, NB, HN, T]), ALU.mult).then_inc(s_hc, 1)

            def make_u(g, par, e):
                need(pool, s_sigu, NC * g + e + 1)
                need(pool, s_skip, NC * (g - 2) + e + 1)
                nc.gpsimd.tensor_tensor(u[:, par, e, :], acc[:, :], sig_u[:, :], ALU.mult).then_inc(s_u, 1)

            def silu_z(g, par, c):
                need(pool, s_sigz, NC * g + c + 1)
                nc.gpsimd.tensor_tensor(sig_z[:, c % 2, :], sig_z[:, c % 2, :], z_c[:, c % 2, :],
                                        ALU.mult).then_inc(s_w, 1)

            def make_xdt(g, par, c):
                if pool_makes_xdt(c):
                    need(pool, s_dt, NC * g + c + 1)
                    nc.gpsimd.tensor_tensor(dtx[:, 1, :], dtx[:, 0, :], u[:, par, c, :], ALU.mult).then_inc(s_xdt, 1)

            def add_residual(g):
                need(pool, s_xrl, 16 * (g + 1))
                for b in range(BG):
                    need(pool, s_og, BG * g + b + 1)
                    nc.gpsimd.tensor_tensor(x_res[:, b, :], x_res[:, b, :], gate[:, b, :],
                                            ALU.add).then_inc(s_res, 1)

            pool.wait_ge(s_ada_mm, 1)
            nc.gpsimd.memset(dec[:, :, :, :, :, :].rearrange("p a c n b t -> p (a c n b t)"), 0.0).then_inc(s_zeroed, 1)

            def step(g, par, c):
                item(g, par, c, 0, weight_states, 0)
                if c == 3 and exists(g - 1):
                    add_residual(g - 1)
                item(g, par, c, 11, make_u)
                item(g, par, c, -1, silu_z)
                item(g, par, c, 3, make_xdt)
                item(g, par, c, 0, weight_states, 1)

            over_groups(pool, step)


SMALL = 8


def columns(vector, parts):
    return vector.reshape(parts, P).T


def kernel(x, cond_2048, L0_cond_ln_g, L0_cond_ln_b, L0_cond_ada_w, L0_cond_ada_b, L0_cond_in_proj_w, L0_cond_conv_w,
           L0_cond_conv_b, L0_cond_x_proj_w, L0_cond_dt_proj_w, L0_cond_dt_proj_b, L0_cond_A_log, L0_cond_D_param,
           L0_cond_out_proj_w):
    import numpy as np
    import concourse.bacc as bacc
    from concourse.bass_utils import run_bass_kernel_spmd

    (x, cond, ln_g, ln_b, ada_w, ada_b, in_w, conv_w, conv_b, x_w, dt_w, dt_b, a_log, d_param, out_w) = [
        np.asarray(a) for a in
        (x, cond_2048, L0_cond_ln_g, L0_cond_ln_b, L0_cond_ada_w, L0_cond_ada_b, L0_cond_in_proj_w, L0_cond_conv_w,
         L0_cond_conv_b, L0_cond_x_proj_w, L0_cond_dt_proj_w, L0_cond_dt_proj_b, L0_cond_A_log, L0_cond_D_param,
         L0_cond_out_proj_w)]
    D, DI = x.shape[2], in_w.shape[0] // 2
    kd, nch, kc = D // P, DI // P, cond.shape[1] // P
    arrays = {
        "x": x,
        "c_t": cond.T.reshape(kc, P, cond.shape[0]),
        "ln_g": columns(ln_g, kd),
        "ln_b": columns(ln_b, kd),
        "ada_wt": ada_w.T.reshape(kc, P, 3 * D),
        "ada_b_col": columns(ada_b[0:2 * D], 2 * kd),
        "ada_b_gate": ada_b[2 * D:].reshape(1, D),
        "in_wt": in_w.T,
        "conv_w": conv_w.reshape(nch, P, -1).transpose(1, 0, 2),
        "conv_b": columns(conv_b, nch),
        "xproj_wt": x_w.T.reshape(nch, P, -1),
        "dt_wt": dt_w.T,
        "dt_b": dt_b.reshape(1, DI),
        "a_log": a_log.reshape(nch, P // CB, CB, Q, -1).transpose(3, 2, 0, 1, 4).reshape(P, nch, P // CB, -1),
        "d_param": columns(d_param, nch),
        "out_wt": out_w.T,
        "eye": np.eye(P, dtype=np.float32),
        "eye_blocks": np.tile(np.eye(CB, dtype=np.float32), (Q, 1)),
    }
    arrays = {name: np.ascontiguousarray(a) for name, a in arrays.items()}
    nc = bacc.Bacc("TRN2", target_bir_lowering=False, num_devices=1)
    args = [nc.dram_tensor(name, a.shape, mybir.dt.from_np(a.dtype), kind="ExternalInput").ap()
            for name, a in arrays.items()]
    out = nc.dram_tensor("out", x.shape, mybir.dt.float32, kind="ExternalOutput").ap()
    mamba_block(nc, *args, out)
    got = run_bass_kernel_spmd(nc, [arrays], core_ids=[0])
    return got.results[0]["out"]
```
